# Optimizing a Trainium2 kernel written in Bass

```python
import numpy as np
import jax
import jax.numpy as jnp

def _softmax(x, axis=-1):
    return jax.nn.softmax(x, axis=axis)

def _gelu(x):
    return jax.nn.gelu(x, approximate=True)

def _silu(x):
    return jax.nn.silu(x)

def _sigmoid(x):
    return jax.nn.sigmoid(x)

def _layernorm(x, axis=-1, eps=1e-05):
    m = jnp.mean(x, axis=axis, keepdims=True)
    v = jnp.var(x, axis=axis, keepdims=True)
    return (x - m) / jnp.sqrt(v + eps)

def _scatter_add(tgt, idx, src, axis=0):
    return tgt.at[idx].add(src)

def _segment_sum(src, seg, n):
    return jax.ops.segment_sum(src, seg, n)
kernel_name = 'mk_hybrid_d1_jaxref_r8_bb3456'

def setup_inputs(seed: int=0):
    np.random.seed(seed)
    _w = jnp.asarray

    def _L0_attn_a_setup():
        import jax, jax.numpy as jnp
        import numpy as np
        H = 512
        D = H // 4
        key = jax.random.key(seed)
        k1, k2, k3, k4, k5 = jax.random.split(key, 5)
        x = jax.random.normal(k1, (4, 512, H), dtype=jnp.float32)
        s_in = 1.0 / np.sqrt(H)
        Wqkv = jax.random.normal(k2, (H, 3 * D), dtype=jnp.float32) * s_in
        bqkv = jax.random.normal(k3, (3 * D,), dtype=jnp.float32) * 0.01
        Wo = jax.random.normal(k4, (D, H), dtype=jnp.float32) * (1.0 / np.sqrt(D))
        bo = jax.random.normal(k5, (H,), dtype=jnp.float32) * 0.01
        return {'x': x, 'Wqkv': Wqkv, 'bqkv': bqkv, 'Wo': Wo, 'bo': bo}
    _L0_attn_a_in = _L0_attn_a_setup()

    def _L0_attn_b_setup():
        import jax, jax.numpy as jnp
        import numpy as np
        import math
        B, S, D = (1, 256, 512)
        H, KV, HD = (32, 8, 128)
        GROUPS = H // KV
        SYS_LEN, IMG_LEN = (35, 72)
        ENH, SUP = (1.5, 0.5)
        ROPE_BASE = 10000.0

        def _rope_cos_sin(seq_len, dtype):
            inv_freq = 1.0 / ROPE_BASE ** (jnp.arange(0, HD, 2, dtype=jnp.float32) / HD)
            pos = jnp.arange(seq_len, dtype=jnp.float32)
            freqs = pos[:, None] * inv_freq[None, :]
            emb = jnp.concatenate([freqs, freqs], axis=-1)
            return (jnp.cos(emb).astype(dtype), jnp.sin(emb).astype(dtype))

        def _rotate_half(x):
            x1, x2 = (x[..., :HD // 2], x[..., HD // 2:])
            return jnp.concatenate([-x2, x1], axis=-1)
        key = jax.random.key(seed)
        ks = jax.random.split(key, 5)
        scale = 0.02
        return {'hidden_states': jax.random.normal(ks[0], (B, S, D), dtype=jnp.float32), 'wq': jax.random.normal(ks[1], (H * HD, D), dtype=jnp.float32) * scale, 'wk': jax.random.normal(ks[2], (KV * HD, D), dtype=jnp.float32) * scale, 'wv': jax.random.normal(ks[3], (KV * HD, D), dtype=jnp.float32) * scale, 'wo': jax.random.normal(ks[4], (D, H * HD), dtype=jnp.float32) * scale}
    _L0_attn_b_in = _L0_attn_b_setup()

    def _L0_ffn_setup():
        import jax, jax.numpy as jnp
        import numpy as np
        HIDDEN = 512
        INTER = 1376

        def _ternary_quantize(w):
            scale = jnp.mean(jnp.abs(w))
            return jnp.clip(jnp.round(w / scale), -1.0, 1.0) * scale
        key = jax.random.key(seed)
        kx, kg, ku, kd = jax.random.split(key, 4)
        x = jax.random.normal(kx, (2, 256, HIDDEN), dtype=jnp.float32)
        w_gate = _ternary_quantize(jax.random.normal(kg, (INTER, HIDDEN), dtype=jnp.float32) * 0.02)
        w_up = _ternary_quantize(jax.random.normal(ku, (INTER, HIDDEN), dtype=jnp.float32) * 0.02)
        w_down = _ternary_quantize(jax.random.normal(kd, (HIDDEN, INTER), dtype=jnp.float32) * 0.02)
        return {'x': x, 'w_gate': w_gate, 'w_up': w_up, 'w_down': w_down}
    _L0_ffn_in = _L0_ffn_setup()
    _d = {'L0_attn_a_x': _L0_attn_a_in['x'], 'L0_attn_a_Wqkv': _L0_attn_a_in['Wqkv'], 'L0_attn_a_bqkv': _L0_attn_a_in['bqkv'], 'L0_attn_a_Wo': _L0_attn_a_in['Wo'], 'L0_attn_a_bo': _L0_attn_a_in['bo'], 'L0_attn_b_wq': _L0_attn_b_in['wq'], 'L0_attn_b_wk': _L0_attn_b_in['wk'], 'L0_attn_b_wv': _L0_attn_b_in['wv'], 'L0_attn_b_wo': _L0_attn_b_in['wo'], 'L0_ffn_w_gate': _L0_ffn_in['w_gate'], 'L0_ffn_w_up': _L0_ffn_in['w_up'], 'L0_ffn_w_down': _L0_ffn_in['w_down']}
    _x0 = _d['L0_attn_a_x']
    _d['L0_attn_a_x'] = jax.random.normal(jax.random.fold_in(jax.random.key(seed), 1), (2, 512, 512), dtype=_x0.dtype)
    del _x0
    return _d

def reference(L0_attn_a_x, L0_attn_a_Wqkv, L0_attn_a_bqkv, L0_attn_a_Wo, L0_attn_a_bo, L0_attn_b_wq, L0_attn_b_wk, L0_attn_b_wv, L0_attn_b_wo, L0_ffn_w_gate, L0_ffn_w_up, L0_ffn_w_down):

    def _L0_attn_a_ref(x, Wqkv, bqkv, Wo, bo):
        import jax, jax.numpy as jnp
        import numpy as np
        H = 512
        D = H // 4
        B, S, C = x.shape
        d = C // 4
        qkv = jnp.einsum('bsc,cf->bsf', x, Wqkv) + bqkv
        qkv = qkv.reshape(B, S, 3, d)
        q, k, v = (qkv[:, :, 0], qkv[:, :, 1], qkv[:, :, 2])
        scale = 1.0 / jnp.sqrt(jnp.float32(d)).astype(x.dtype)
        attn = jnp.einsum('bqd,bkd->bqk', q, k) * scale
        attn = jax.nn.softmax(attn, axis=-1)
        out = jnp.einsum('bqk,bkd->bqd', attn, v)
        return jnp.einsum('bqd,dc->bqc', out, Wo) + bo

    def _L0_attn_b_ref(hidden_states, wq, wk, wv, wo):
        import jax, jax.numpy as jnp
        import numpy as np
        import math
        B, S, D = (1, 256, 512)
        H, KV, HD = (32, 8, 128)
        GROUPS = H // KV
        SYS_LEN, IMG_LEN = (35, 72)
        ENH, SUP = (1.5, 0.5)
        ROPE_BASE = 10000.0

        def _rope_cos_sin(seq_len, dtype):
            inv_freq = 1.0 / ROPE_BASE ** (jnp.arange(0, HD, 2, dtype=jnp.float32) / HD)
            pos = jnp.arange(seq_len, dtype=jnp.float32)
            freqs = pos[:, None] * inv_freq[None, :]
            emb = jnp.concatenate([freqs, freqs], axis=-1)
            return (jnp.cos(emb).astype(dtype), jnp.sin(emb).astype(dtype))

        def _rotate_half(x):
            x1, x2 = (x[..., :HD // 2], x[..., HD // 2:])
            return jnp.concatenate([-x2, x1], axis=-1)
        bsz, q_len, _ = hidden_states.shape
        dt = hidden_states.dtype
        q = (hidden_states @ wq.T).reshape(bsz, q_len, H, HD).transpose(0, 2, 1, 3)
        k = (hidden_states @ wk.T).reshape(bsz, q_len, KV, HD).transpose(0, 2, 1, 3)
        v = (hidden_states @ wv.T).reshape(bsz, q_len, KV, HD).transpose(0, 2, 1, 3)
        cos, sin = _rope_cos_sin(q_len, dt)
        q = q * cos + _rotate_half(q) * sin
        k = k * cos + _rotate_half(k) * sin
        k = jnp.repeat(k, GROUPS, axis=1)
        v = jnp.repeat(v, GROUPS, axis=1)
        scores = jnp.einsum('bhqd,bhkd->bhqk', q, k) / math.sqrt(HD)
        kpos = jnp.arange(q_len)
        key_scale = jnp.where(kpos < SYS_LEN, SUP, jnp.where(kpos < SYS_LEN + IMG_LEN, ENH, 1.0)).astype(dt)
        qpos = jnp.arange(q_len)
        row_sel = (qpos >= SYS_LEN + IMG_LEN)[:, None]
        scale = jnp.where(row_sel, key_scale[None, :], jnp.ones((), dt))
        scores = scores * scale
        causal = jnp.where(qpos[:, None] >= kpos[None, :], 0.0, jnp.finfo(jnp.float32).min)
        scores = scores + causal.astype(dt)
        probs = jax.nn.softmax(scores.astype(jnp.float32), axis=-1).astype(dt)
        attn = jnp.einsum('bhqk,bhkd->bhqd', probs, v)
        attn = attn.transpose(0, 2, 1, 3).reshape(bsz, q_len, H * HD)
        return attn @ wo.T

    def _L0_ffn_ref(x, w_gate, w_up, w_down):
        import jax, jax.numpy as jnp
        import numpy as np
        HIDDEN = 512
        INTER = 1376

        def _ternary_quantize(w):
            scale = jnp.mean(jnp.abs(w))
            return jnp.clip(jnp.round(w / scale), -1.0, 1.0) * scale
        xf = x.astype(jnp.float32) / 128.0
        gate = jnp.einsum('bsh,ih->bsi', xf, w_gate)
        up = jnp.einsum('bsh,ih->bsi', xf, w_up)
        inter = jax.nn.silu(gate) * up
        inter_q = jnp.trunc(jnp.clip(inter * 128.0, -128.0, 127.0)).astype(jnp.int8)
        down = jnp.einsum('bsi,hi->bsh', inter_q.astype(jnp.float32), w_down)
        out = jnp.trunc(jnp.clip(down * 128.0, -128.0, 127.0)).astype(jnp.int8)
        return out
    x = L0_attn_a_x
    x = x + _L0_attn_a_ref(_layernorm(x, axis=-1), L0_attn_a_Wqkv, L0_attn_a_bqkv, L0_attn_a_Wo, L0_attn_a_bo)
    x = x + _L0_ffn_ref(_layernorm(x, axis=-1), L0_ffn_w_gate, L0_ffn_w_up, L0_ffn_w_down)
    x = x + _L0_attn_b_ref(_layernorm(x, axis=-1), L0_attn_b_wq, L0_attn_b_wk, L0_attn_b_wv, L0_attn_b_wo)
    x = x + _L0_ffn_ref(_layernorm(x, axis=-1), L0_ffn_w_gate, L0_ffn_w_up, L0_ffn_w_down)
    return x

_drawn_inputs = setup_inputs


def setup_inputs(seed=0):
    import zlib

    import numpy as np

    out = dict(_drawn_inputs(seed))
    spreads = {}
    factors = {'L0_attn_a_bqkv': 4.257,
     'L0_attn_a_bo': 5.074,
     'L0_attn_b_wq': 4.118,
     'L0_attn_b_wk': 4.021}
    for name, (base, spread) in spreads.items():
        noise = np.random.default_rng([zlib.crc32(name.encode()), seed]).standard_normal(out[name].shape)
        drawn = base * np.exp(spread * noise) if base else spread * noise
        out[name] = jnp.asarray(drawn.astype(out[name].dtype))
    for name, factor in factors.items():
        out[name] = (out[name] * factor).astype(out[name].dtype)
    return out
```

```python
from contextlib import ExitStack

import numpy as np
import concourse.bass as bass
from concourse import mybir

F32 = mybir.dt.float32
F32R = mybir.dt.float32r
ALU = mybir.AluOpType
ACT = mybir.ActivationFunctionType
AX_X = mybir.AxisListType.X

P = 128
NB = 2
SEQ = 512
TB = SEQ // P
NT = NB * TB
C = 512
CK = C // P
INTER = 1376
NI = -(-INTER // P)
HEADS, KVH = 32, 8
GH = HEADS // KVH
SYS, IMG = 35, 72
BOOST = SYS + IMG
SCALE = float(1.0 / np.sqrt(np.float32(P)))
EPS = 1e-5
LOWEST = float(np.finfo(np.float32).min)
ROUND = float(3 << 22)
TRI = [0, 1, 3, 6]
PAIRS = 10

A_PIECES = 4
F_PER = 3
B_PER = 10
F_BASE = A_PIECES
B_BASE = F_BASE + F_PER * NI
RAW = 6
B_RAW = 5


def need(eng, sem, count):
    if not (isinstance(count, int) and count <= 0):
        eng.wait_ge(sem, count)


def build(nc, x_in, weights, bqkv, bo, rope_q, rope_k, masks, out):
    with ExitStack() as ctx:
        place = [nc.sbuf_base]

        def sb(name, shape, dt=F32):
            size = int(np.prod(shape[1:])) * 4
            t = nc.alloc_sbuf_tensor_at(name, shape, dt, offset=place[0])
            place[0] += -(-size // 32) * 32
            return t

        def sem(name):
            return ctx.enter_context(nc.semaphore(name))

        place[0] = -(-place[0] // 32) * 32
        x = sb("x", [P, NT, C])
        xn_hi = sb("xn_hi", [P, CK, NT * P], F32R)
        xn_lo = sb("xn_lo", [P, CK, NT * P], F32R)
        ident = sb("ident", [P, P])
        raw = sb("raw", [P, RAW, C])
        stats = sb("stats", [P, NT, 6])
        mv = sb("mv", [P, NT, 2])
        vare = sb("vare", [P, NT, 1])
        rstd = sb("rstd", [P, NT, 1])
        mhalf = sb("mhalf", [P, 1])
        xn_tmp = sb("xn_tmp", [P, 2, C])
        start = place[0]

        wgu_hi = sb("wgu_hi", [P, 2, 2, CK, P], F32R)
        wgu_lo = sb("wgu_lo", [P, 2, 2, CK, P], F32R)
        after_gu = place[0]
        wd_hi = sb("wd_hi", [P, NI, C], F32R)
        wd_lo = sb("wd_lo", [P, NI, C], F32R)
        inner = sb("inner", [P, NI, NB, SEQ], F32R)
        f_sil = sb("f_sil", [P, 2, 512])
        f_z = sb("f_z", [P, 2, 512])
        f_abs = sb("f_abs", [P, 2, 512])
        f_sgn = sb("f_sgn", [P, 2, 512])
        f_rnd = sb("f_rnd", [P, 2, 512])
        f_off = sb("f_off", [P, 2, 512])
        f_val = sb("f_val", [P, 2, 512])
        top = place[0]

        place[0] = after_gu
        aw_hi = sb("aw_hi", [P, 4, CK, P], F32R)
        aw_lo = sb("aw_lo", [P, 4, CK, P], F32R)
        a_bias = sb("a_bias", [P, 3])
        a_bo = sb("a_bo", [P, C])
        aqk_hi = sb("aqk_hi", [P, NB, 2, SEQ], F32R)
        aqk_lo = sb("aqk_lo", [P, NB, 2, SEQ], F32R)
        a_vT = sb("a_vT", [P, NB, SEQ])
        av_hi = sb("av_hi", [P, NB, TB, P], F32R)
        av_lo = sb("av_lo", [P, NB, TB, P], F32R)
        a_p = sb("a_p", [P, NB, TB, SEQ])
        a_nmax = sb("a_nmax", [P, NT])
        a_sum = sb("a_sum", [P, NT])
        a_rec = sb("a_rec", [P, NT])
        apt_hi = sb("apt_hi", [P, 2, SEQ], F32R)
        apt_lo = sb("apt_lo", [P, 2, SEQ], F32R)
        ao_hi = sb("ao_hi", [P, NB, SEQ], F32R)
        ao_lo = sb("ao_lo", [P, NB, SEQ], F32R)
        assert place[0] <= top

        place[0] = start
        wo_hi = sb("wo_hi", [P, GH, C], F32R)
        wo_lo = sb("wo_lo", [P, GH, C], F32R)
        wq_hi = sb("wq_hi", [P, GH, CK, P], F32R)
        wq_lo = sb("wq_lo", [P, GH, CK, P], F32R)
        wkv_hi = sb("wkv_hi", [P, CK, 2 * P], F32R)
        wkv_lo = sb("wkv_lo", [P, CK, 2 * P], F32R)
        qT_hi = sb("qT_hi", [P, NB, GH, SEQ], F32R)
        qT_lo = sb("qT_lo", [P, NB, GH, SEQ], F32R)
        k1_hi = sb("k1_hi", [P, NB, 2 * P], F32R)
        k1_lo = sb("k1_lo", [P, NB, 2 * P], F32R)
        k2_hi = sb("k2_hi", [P, NB, SEQ], F32R)
        k2_lo = sb("k2_lo", [P, NB, SEQ], F32R)
        v_hi = sb("v_hi", [P, NB, TB, P], F32R)
        v_lo = sb("v_lo", [P, NB, TB, P], F32R)
        prob0 = sb("prob0", [P, GH, 3 * P])
        prob1 = sb("prob1", [P, GH, 4 * P])
        pt_hi = sb("pt_hi", [P, 2, 512], F32R)
        pt_lo = sb("pt_lo", [P, 2, 512], F32R)
        o_hi = sb("o_hi", [P, GH, P], F32R)
        o_lo = sb("o_lo", [P, GH, P], F32R)
        rq_cos = sb("rq_cos", [P, 2, 512])
        rq_sin = sb("rq_sin", [P, 2, 512])
        rk_cos = sb("rk_cos", [P, TB, P])
        rk_sin = sb("rk_sin", [P, TB, P])
        k2_tmp = sb("k2_tmp", [P, P])
        tab_q = sb("tab_q", [P, 2, SEQ])
        tab_k = sb("tab_k", [P, 2, TB, P])
        tab_m = sb("tab_m", [P, 512 + 2 * P])
        nmax = sb("nmax", [P, TB, GH])
        esum = sb("esum", [P, TB, GH])
        rec = sb("rec", [P, TB, GH])
        assert max(place[0], top) <= nc.sbuf_usable_end
        causal = tab_m[:, 0:512]
        rowscale = tab_m[:, 512:640]
        colscale = tab_m[:, 640:768]
        prob = [prob0, prob1]

        bank = [ctx.enter_context(nc.psum_tensor(f"bank{i}", [P, 512], F32)) for i in range(8)]

        x_in_sem = [sem(f"x_in_{t}") for t in range(NT)]
        ident_set = sem("ident_set")
        ident_ready = sem("ident_ready")
        small_in = sem("small_in")
        table_in = sem("table_in")
        ld_a = [sem(f"ld_a{j}") for j in range(A_PIECES)]
        ld_f = [[sem(f"ld_f{n}_{j}") for j in range(RAW)] for n in range(2)]
        ld_b = [sem(f"ld_b{j}") for j in range(B_RAW)]
        hi_done = sem("hi_done")
        lo_done = sem("lo_done")
        wd_h = sem("wd_h")
        wd_done = sem("wd_done")
        stored = sem("stored")
        ln_stat, ln_aggr, ln_eps, ln_rstd = sem("ln_stat"), sem("ln_aggr"), sem("ln_eps"), sem("ln_rstd")
        ln_xn, ln_tr, ln_hi, ln_lo = sem("ln_xn"), sem("ln_tr"), sem("ln_hi"), sem("ln_lo")
        a_proj, a_qk, a_lo, a_vt, a_vtr, a_vh, a_v = (sem(n) for n in (
            "a_proj", "a_qk", "a_lo", "a_vt", "a_vtr", "a_vh", "a_v"))
        a_s, a_min, a_exp, a_recd, a_norm = (sem(n) for n in ("a_s", "a_min", "a_exp", "a_recd", "a_norm"))
        a_pt, a_pth, a_ptl, a_pv, a_oh, a_ol, a_y, a_res, a_bod = (sem(n) for n in (
            "a_pt", "a_pth", "a_ptl", "a_pv", "a_oh", "a_ol", "a_y", "a_res", "a_bod"))
        f_gate, f_up, f_silu, f_zd, f_absd, f_sgnd, f_rndd, f_offd, f_vald, f_sgd, f_qd = (
            sem(n) for n in ("f_gate", "f_up", "f_silu", "f_zd", "f_absd", "f_sgnd", "f_rndd",
                             "f_offd", "f_vald", "f_sgd", "f_qd"))
        f_y, f_res = sem("f_y"), sem("f_res")
        kv_done, kv_rot, kv_rope, kt_done, kh_done, k2_scaled, k2_round, k_done, vh_done, v_done = (
            sem(n) for n in ("kv_done", "kv_rot", "kv_rope", "kt_done", "kh_done", "k2_scaled",
                             "k2_round", "k_done", "vh_done", "v_done"))
        k1_zero = sem("k1_zero")
        q_done, q_read, q_sum, q_hi, q_lo = (
            sem(n) for n in ("q_done", "q_read", "q_sum", "q_hi", "q_lo"))
        s_done, s_scaled, min_done, exp_done, rec_done, norm_done = (
            sem(n) for n in ("s_done", "s_scaled", "min_done", "exp_done", "rec_done", "norm_done"))
        pt_done, pth_done, ptl_done, o_done, oh_done, ol_done, y_done, y_res = (
            sem(n) for n in ("pt_done", "pth_done", "ptl_done", "o_done", "oh_done", "ol_done",
                             "y_done", "y_res"))

        lo_f = [A_PIECES, A_PIECES + 2 * NI + B_PER * KVH]
        lo_b = A_PIECES + 2 * NI

        def consumed(s):
            if s < A_PIECES:
                return s, (lo_done, s + 1)
            n = 0 if s < B_BASE else 1
            if n and s < B_BASE + B_PER * KVH:
                g, j = divmod(s - B_BASE, B_PER)
                return j % B_RAW, (lo_done, lo_b + B_PER * g + j + 1)
            i, j = divmod(s - (F_BASE if not n else B_BASE + B_PER * KVH), F_PER)
            done = (wd_done, NI * n + i + 1) if j == 2 else (lo_done, lo_f[n] + 2 * i + j + 1)
            return F_PER * (i % 2) + j, done

        def before(s):
            slot = consumed(s)[0]
            for r in range(s - 1, -1, -1):
                if consumed(r)[0] == slot:
                    return consumed(r)[1]
            return None

        block = ctx.enter_context(nc.Block())

        @block.sync
        def _(sp):
            def load(s, piece, slot, sem_):
                w = before(s)
                if w:
                    sp.wait_ge(*w)
                sp.dma_start(raw[:, slot, :], weights[piece]).then_inc(sem_, 16)

            for s in range(A_PIECES):
                load(s, s, s, ld_a[s])

            def ffn(n):
                base = F_BASE if n == 0 else B_BASE + B_PER * KVH

                def chunk(i):
                    for j in range(F_PER):
                        load(base + F_PER * i + j, F_BASE + F_PER * i + j, F_PER * (i % 2) + j,
                             ld_f[n][F_PER * (i % 2) + j])

                chunk(0)
                chunk(1)
                with sp.Fori(1, NI // 2) as p:
                    for par in range(2):
                        i = 2 * p + par
                        for j in range(F_PER):
                            if j == 2:
                                sp.wait_ge(wd_done, NI * n + i - 1)
                            else:
                                sp.wait_ge(lo_done, lo_f[n] + 2 * i - 4 + j + 1)
                            sp.dma_start(raw[:, F_PER * par + j, :], weights[F_BASE + F_PER * i + j])\
                              .then_inc(ld_f[n][F_PER * par + j], 16)
                chunk(NI - 1)

            ffn(0)
            for j in range(B_PER):
                load(B_BASE + j, B_BASE + j, j % B_RAW, ld_b[j % B_RAW])
            with sp.Fori(1, KVH) as g:
                for j in range(B_PER):
                    sp.wait_ge(lo_done, lo_b + B_PER * g + j - B_RAW + 1)
                    sp.dma_start(raw[:, j % B_RAW, :], weights[B_BASE + B_PER * g + j])\
                      .then_inc(ld_b[j % B_RAW], 16)
            ffn(1)

            out_t = out.rearrange("b (t p) c -> p (b t) c", p=P)
            for t in range(NT):
                sp.wait_ge(f_res, NT + t + 1)
                sp.dma_start(out_t[:, t, :], x[:, t, :]).then_inc(stored, 16)
            sp.wait_ge(stored, 16 * NT)


        def unit_order(b, first, last, group_first, group_last):
            fill = {
                (0, 0): [("kv", 1, 0)], (0, 1): [("y", -1, 2)], (0, 2): [("kv", 1, 1)],
                (0, 3): [("kv", 1, 2)],
                (1, 0): [("kv", 1, 3), ("kv_out", 1, 0)], (1, 1): [("y", -1, 3)],
                (1, 2): [("q", 1, (0, 0))], (1, 3): [("kt", 1, 0), ("q", 1, (0, 1))],
                (2, 0): [("q", 1, (1, 0))], (2, 1): [("q", 1, (1, 1))], (2, 2): [("y", 0, 0)],
                (2, 3): [("q", 1, (2, 0))],
                (3, 0): [("q", 1, (2, 1))], (3, 1): [("y", 0, 1)], (3, 2): [("q", 1, (3, 0))],
                (3, 3): [("q", 1, (3, 1))],
            }
            if b == 0:
                if not group_first:
                    for i, at in enumerate(((1, 1), (1, 2), (1, 3), (2, 0))):
                        fill[at].append(("w", 0, 6 + i))
                if not group_last:
                    fill[(2, 1)].append(("w", 2, 0))
                    fill[(2, 3)].append(("w", 2, 1))
            elif not group_last:
                for i in range(4):
                    fill[(0, i)].append(("w", 1, 2 + i))
            order = []
            for k in range(TB):
                back, tile = (0, k - 1) if k else (-1, TB - 1)
                for h in range(GH):
                    order.append(("s", 0, (k, h)))
                    order += fill[(k, h)]
                    if 1 <= h <= tile + 1:
                        order.append(("pv", back, (tile, h - 1)))
                    if (k, h) == (1, 0):
                        order.append(("pv", -1, (TB - 1, TB - 1)))
                    if h <= tile:
                        order.append(("t", back, (tile, h)))
            keep = []
            for what, d, arg in order:
                if d == -1 and first:
                    continue
                if d == 1 and last and what != "w":
                    continue
                keep.append((what, d, arg))
            return keep

        FIRST_UNIT = [("kv", 0, t) for t in range(TB)] + [("kv_out", 0, 0)] \
            + [("q", 0, (0, 0)), ("q", 0, (0, 1)), ("kt", 0, 0)] \
            + [("q", 0, (h, half)) for h in range(1, GH) for half in range(2)]
        LAST_TURN = [("s_end", 0, 0), ("t", 0, (3, 0)), ("y", 0, 2), ("t", 0, (3, 1)),
                     ("pv", 0, (3, 0)), ("pv", 0, (3, 1)), ("t", 0, (3, 2)), ("t", 0, (3, 3)),
                     ("pv", 0, (3, 2)), ("pv", 0, (3, 3)), ("y", 0, 3)]

        def walk(eng, run):
            for what, _, arg in FIRST_UNIT:
                run(what, 0, 0, arg, (True, False))

            def group(g, group_first=False, group_last=False):
                for b in range(NB):
                    first, last = group_first and b == 0, group_last and b == 1
                    for what, d, arg in unit_order(b, first, last, group_first, group_last):
                        if what == "w":
                            run(what, g + (1 if arg < 6 else 0), 0, arg, (first, last))
                        else:
                            run(what, g + (b + d) // NB, (b + d) % NB, arg, (first, last))

            group(0, group_first=True)
            with eng.Fori(1, KVH - 1) as g:
                group(g)
            group(KVH - 1, group_last=True)
            for what, _, arg in LAST_TURN:
                run(what, KVH - 1, NB - 1, arg, (False, True))

        def w_parts(j):
            if j < 2:
                return tuple(w[:, 2 * j:2 * j + 2, :].rearrange("p c d -> p (c d)") for w in (wkv_hi, wkv_lo))
            if j < 6:
                return tuple(w[:, j - 2].rearrange("p c d -> p (c d)") for w in (wq_hi, wq_lo))
            return wo_hi[:, j - 6, :], wo_lo[:, j - 6, :]

        def gu_part(w, par, j):
            return w[:, par, j].rearrange("p c d -> p (c d)")

        def a_part(w, j):
            return w[:, j].rearrange("p c d -> p (c d)")

        f_steps = NB * NI + NT

        @block.gpsimd
        def _(pool):
            pool.memset(ident[:], 0.0).then_inc(ident_set, 1)
            pool.memset(mhalf[:], -0.5).then_inc(ident_set, 1)
            pool.wait_ge(ident_set, 2)
            pool.affine_select(out=ident[:], in_=ident[:], compare_op=ALU.not_equal, fill=1.0, base=0,
                               pattern=[[-1, P]], channel_multiplier=1).then_inc(ident_ready, 1)

            def split_lo(count, slot, hi, lo):
                pool.wait_ge(hi_done, count)
                pool.tensor_tensor(lo, raw[:, slot, :], hi.bitcast(F32), ALU.subtract)\
                    .then_inc(lo_done, 1)

            def norm(n):
                for t in range(NT):
                    pool.wait_ge(ln_eps, NT * n + t + 1)
                    pool.tensor_tensor(rstd[:, t, :], vare[:, t, :], mhalf[:], ALU.pow)\
                        .then_inc(ln_rstd, 1)

            def signs(count, slot):
                pool.wait_ge(f_vald, count)
                pool.tensor_tensor(f_val[:, slot, :], f_val[:, slot, :], f_sgn[:, slot, :], ALU.mult)\
                    .then_inc(f_sgd, 1)

            def ffn(n):
                def gu_lo(i, par):
                    for j in range(2):
                        split_lo(lo_f[n] + 2 * i + j + 1, F_PER * par + j,
                                 gu_part(wgu_hi, par, j), gu_part(wgu_lo, par, j))

                def chunk(i, par, last=False):
                    if not last:
                        gu_lo(i + 1, 1 - par)
                    for b in range(NB):
                        signs(f_steps * n + NB * i + b + 1, b)

                gu_lo(0, 0)
                norm(1 + 2 * n)
                chunk(0, 0)
                chunk(1, 1)
                with pool.Fori(1, NI // 2) as p:
                    for par in range(2):
                        chunk(2 * p + par, par)
                chunk(NI - 1, 0, last=True)
                for t in range(NT):
                    signs(f_steps * n + NB * NI + t + 1, t % 2)

            def run(what, g, b, arg, flags):
                u = NB * g + b
                if what == "w":
                    split_lo(lo_b + B_PER * g + arg + 1, arg % B_RAW, *w_parts(arg))
                elif what == "kv_out":
                    pool.wait_ge(kv_rot, u + 1)
                    pool.tensor_tensor(rk_cos[:], rk_cos[:], rk_sin[:], ALU.add).then_inc(kv_rope, 1)
                elif what == "q" and arg[1] == 1:
                    h = arg[0]
                    pool.wait_ge(q_read, GH * u + h + 1)
                    pool.tensor_tensor(rq_cos[:, h % 2, :], rq_cos[:, h % 2, :], rq_sin[:, h % 2, :],
                                       ALU.add).then_inc(q_sum, 1)
                    pool.wait_ge(q_hi, GH * u + h + 1)
                    pool.tensor_tensor(qT_lo[:, b, h, :], rq_cos[:, h % 2, :],
                                       qT_hi[:, b, h, :].bitcast(F32), ALU.subtract).then_inc(q_lo, 1)

            norm(0)
            for j in range(A_PIECES):
                split_lo(j + 1, j, a_part(aw_hi, j), a_part(aw_lo, j))
            pool.wait_ge(small_in, 32)
            for t in range(NT):
                pool.wait_ge(a_res, t + 1)
                pool.tensor_tensor(x[:, t, :], x[:, t, :], a_bo[:], ALU.add).then_inc(a_bod, 1)
            ffn(0)
            for j in range(B_PER):
                run("w", 0, 0, j, None)
            norm(2)
            walk(pool, run)
            ffn(1)

        @block.scalar
        def _(act):
            x_t = x_in.rearrange("b (t p) c -> p (b t) c", p=P)
            for t in range(NT):
                act.dma_start(x[:, t, :], x_t[:, t, :]).then_inc(x_in_sem[t], 16)
            act.dma_start(a_bias[:], bqkv).then_inc(small_in, 16)
            act.dma_start(a_bo[:], bo).then_inc(small_in, 16)

            def split_hi(slot, ready, count, hi):
                act.wait_ge(ready, count)
                act.activation(hi, raw[:, slot, :], ACT.Copy).then_inc(hi_done, 1)

            def norm(n):
                for t in range(NT):
                    act.wait_ge(ln_tr, NT * n + t + 1)
                    act.activation(xn_hi[:, :, P * t:P * t + P],
                                   bank[6 + t % 2][:].rearrange("p (c q) -> p c q", c=CK), ACT.Copy)\
                       .then_inc(ln_hi, 1)

            for j in range(A_PIECES):
                split_hi(j, ld_a[j], 16, a_part(aw_hi, j))
            norm(0)
            act.wait_ge(small_in, 32)
            for b in range(NB):
                for j in range(2):
                    act.wait_ge(a_proj, 3 * b + j + 1)
                    act.activation(aqk_hi[:, b, j, :], bank[j][:], ACT.Identity,
                                   bias=a_bias[:, j:j + 1]).then_inc(a_qk, 1)
                act.wait_ge(a_proj, 3 * b + 3)
                act.activation(a_vT[:, b, :], bank[2][:], ACT.Identity, bias=a_bias[:, 2:3])\
                   .then_inc(a_vt, 1)
                act.wait_ge(a_vtr, b + 1)
                act.activation(av_hi[:, b].rearrange("p c d -> p (c d)"), bank[3][:], ACT.Copy)\
                   .then_inc(a_vh, 1)
            for t in range(NT):
                b, qb = divmod(t, TB)
                act.wait_ge(a_min, t + 1)
                act.activation(a_p[:, b, qb, :], a_p[:, b, qb, :], ACT.Exp, bias=a_nmax[:, t:t + 1],
                               scale=-1.0, accum_out=a_sum[:, t:t + 1]).then_inc(a_exp, 1)
                act.wait_ge(a_recd, t + 1)
                act.activation(a_p[:, b, qb, :], a_p[:, b, qb, :], ACT.Copy,
                               scale=a_rec[:, t:t + 1]).then_inc(a_norm, 1)
            for b in range(NB):
                for kt in range(TB):
                    act.wait_ge(a_pt, TB * b + kt + 1)
                    act.activation(apt_hi[:, kt % 2, :], bank[6 + kt % 2][:], ACT.Copy).then_inc(a_pth, 1)
                act.wait_ge(a_pv, b + 1)
                act.activation(ao_hi[:, b, :], bank[0][:], ACT.Copy).then_inc(a_oh, 1)

            def magnitude(slot, src, scale):
                act.activation(f_abs[:, slot, :], src, ACT.Abs, scale=scale).then_inc(f_absd, 1)
                act.activation(f_sgn[:, slot, :], src, ACT.Sign).then_inc(f_sgnd, 1)

            def ffn(n):
                def gu_hi(i, par):
                    loads = i // 2 + 1 if isinstance(i, int) else None
                    for j in range(2):
                        count = 16 * loads if loads is not None else (i - par) * 8 + 16
                        split_hi(F_PER * par + j, ld_f[n][F_PER * par + j], count, gu_part(wgu_hi, par, j))

                def chunk(i, par, last=False):
                    done = NB * NI * n + NB * i
                    for b in range(NB):
                        act.wait_ge(f_gate, done + b + 1)
                        act.activation(f_sil[:, b, :], bank[2 * b][:], ACT.Silu, scale=1.0 / 128.0)\
                           .then_inc(f_silu, 1)
                        if b == 0 and not last:
                            need(act, f_up, done)
                            gu_hi(i + 1, 1 - par)
                        need(act, f_sgd, f_steps * n + NB * i + b - 1)
                        act.wait_ge(f_zd, done + b + 1)
                        magnitude(b, f_z[:, b, :], 1.0)

                if n:
                    act.wait_ge(y_res, TB * NB * KVH)
                gu_hi(0, 0)
                norm(1 + 2 * n)
                chunk(0, 0)
                chunk(1, 1)
                with act.Fori(1, NI // 2) as p:
                    for par in range(2):
                        chunk(2 * p + par, par)
                chunk(NI - 1, 0, last=True)
                for t in range(NT):
                    act.wait_ge(f_sgd, f_steps * n + NB * NI + t - 1)
                    act.wait_ge(f_y, NT * n + t + 1)
                    magnitude(t % 2, bank[4 + t % 2][:], 128.0)

            def normalize(c, k, h):
                w = P * (k + 1)
                act.wait_ge(rec_done, c + 1)
                act.activation(prob[k % 2][:, h, 0:w], prob[k % 2][:, h, 0:w], ACT.Copy,
                               scale=rec[:, k, h:h + 1]).then_inc(norm_done, 1)

            def run(what, g, b, arg, flags):
                u = NB * g + b
                if what == "w":
                    if arg < 6:
                        if arg < 2:
                            need(act, kv_done, 2 * u)
                        else:
                            need(act, q_done, GH * (u - 1) + arg - 1)
                    else:
                        need(act, y_done, TB * u)
                    split_hi(arg % B_RAW, ld_b[arg % B_RAW], 32 * g + 16 * (arg // B_RAW + 1),
                             w_parts(arg)[0])
                elif what == "kv_out":
                    need(act, o_done, TB * (u - 1) if not isinstance(u, int) or u > 1 else 0)
                    for half in range(2):
                        act.wait_ge(kv_done, 2 * u + half + 1)
                        act.activation(v_hi[:, b, 2 * half:2 * half + 2, :],
                                       bank[half][:].rearrange("p (t n) -> p t n", t=2)[:, :, P:2 * P],
                                       ACT.Copy).then_inc(vh_done, 1)
                elif what == "kt":
                    act.wait_ge(kt_done, u + 1)
                    act.activation(k1_hi[:, b, 0:P], bank[2][:, 0:P], ACT.Copy)
                    act.activation(k2_hi[:, b, P:SEQ], bank[2][:, P:SEQ], ACT.Copy).then_inc(kh_done, 1)
                elif what == "q" and arg[1] == 1:
                    h = arg[0]
                    act.wait_ge(q_sum, GH * u + h + 1)
                    act.activation(qT_hi[:, b, h, :], rq_cos[:, h % 2, :], ACT.Copy).then_inc(q_hi, 1)
                elif what == "s":
                    k, h = arg
                    c = 16 * u + GH * k + h
                    if not (flags[0] and k == 0 and h == 0):
                        normalize(c - 1, k if h else (k - 1) % TB, (h - 1) % GH)
                    w = P * (k + 1)
                    act.wait_ge(min_done, c + 1)
                    act.activation(prob[k % 2][:, h, 0:w], prob[k % 2][:, h, 0:w], ACT.Exp,
                                   bias=nmax[:, k, h:h + 1], scale=-1.0, accum_out=esum[:, k, h:h + 1])\
                       .then_inc(exp_done, 1)
                elif what == "s_end":
                    normalize(16 * u + 15, TB - 1, GH - 1)
                elif what == "t":
                    j = PAIRS * u + TRI[arg[0]] + arg[1]
                    par = (TRI[arg[0]] + arg[1]) % 2
                    act.wait_ge(pt_done, j + 1)
                    act.activation(pt_hi[:, par, :], bank[5 + par][:], ACT.Copy).then_inc(pth_done, 1)
                elif what == "pv" and arg[0] == arg[1]:
                    act.wait_ge(o_done, TB * u + arg[0] + 1)
                    act.activation(o_hi[:].rearrange("p h q -> p (h q)"), bank[7][:], ACT.Copy)\
                       .then_inc(oh_done, 1)

            ffn(0)
            act.wait_ge(f_res, NT)
            act.dma_start(tab_q[:], rope_q).then_inc(table_in, 16)
            act.dma_start(tab_k[:], rope_k).then_inc(table_in, 16)
            act.dma_start(tab_m[:], masks).then_inc(table_in, 16)
            for j in range(B_PER):
                run("w", 0, 0, j, None)
            norm(2)
            walk(act, run)
            ffn(1)

        @block.vector
        def _(dve):
            def norm(n, x_ready):
                def tile(t):
                    x_ready(t)
                    dve.bn_stats(stats[:, t, :], x[:, t, :]).then_inc(ln_stat, 1)
                    dve.wait_ge(ln_stat, NT * n + t + 1)
                    dve.bn_aggr(mv[:, t, :], stats[:, t, :]).then_inc(ln_aggr, 1)
                    dve.wait_ge(ln_aggr, NT * n + t + 1)
                    dve.tensor_scalar(vare[:, t, :], mv[:, t, 1:2], EPS, None, ALU.add).then_inc(ln_eps, 1)

                def center(t):
                    dve.wait_ge(ln_rstd, NT * n + t + 1)
                    need(dve, ln_tr, NT * n + t - 1)
                    dve.tensor_scalar(xn_tmp[:, t % 2, :], x[:, t, :], mv[:, t, 0:1], rstd[:, t, 0:1],
                                      ALU.subtract, ALU.mult).then_inc(ln_xn, 1)

                def lo(t):
                    dve.wait_ge(ln_hi, NT * n + t + 1)
                    dve.tensor_tensor(xn_lo[:, :, P * t:P * t + P],
                                      bank[6 + t % 2][:].rearrange("p (c q) -> p c q", c=CK),
                                      xn_hi[:, :, P * t:P * t + P].bitcast(F32), ALU.subtract)\
                       .then_inc(ln_lo, 1)

                for t in range(NT + 3):
                    if t < NT:
                        tile(t)
                    if 1 <= t < NT + 1:
                        center(t - 1)
                    if t >= 3:
                        lo(t - 3)

            norm(0, lambda t: dve.wait_ge(x_in_sem[t], 16))

            dve.wait_ge(small_in, 32)
            for b in range(NB):
                for j in range(2):
                    dve.wait_ge(a_qk, 2 * b + j + 1)
                    dve.scalar_tensor_tensor(out=aqk_lo[:, b, j, :], in0=bank[j][:],
                                             scalar=a_bias[:, j:j + 1],
                                             in1=aqk_hi[:, b, j, :].bitcast(F32),
                                             op0=ALU.add, op1=ALU.subtract).then_inc(a_lo, 1)
                dve.wait_ge(a_vh, b + 1)
                dve.tensor_tensor(av_lo[:, b].rearrange("p c d -> p (c d)"), bank[3][:],
                                  av_hi[:, b].rearrange("p c d -> p (c d)").bitcast(F32),
                                  ALU.subtract).then_inc(a_v, 1)
            for t in range(NT + 1):
                b, qb = divmod(t, TB)
                if t < NT:
                    dve.wait_ge(a_s, t + 1)
                    dve.tensor_scalar(a_p[:, b, qb, :], bank[4 + t % 2][:], -SCALE, None, ALU.mult,
                                      ALU.min, accum_out=a_nmax[:, t:t + 1]).then_inc(a_min, 1)
                if t:
                    dve.wait_ge(a_exp, t)
                    dve.reciprocal(a_rec[:, t - 1:t], a_sum[:, t - 1:t]).then_inc(a_recd, 1)
            for b in range(NB):
                for kt in range(TB):
                    dve.wait_ge(a_pth, TB * b + kt + 1)
                    dve.tensor_tensor(apt_lo[:, kt % 2, :], bank[6 + kt % 2][:],
                                      apt_hi[:, kt % 2, :].bitcast(F32), ALU.subtract).then_inc(a_ptl, 1)
                dve.wait_ge(a_oh, b + 1)
                dve.tensor_tensor(ao_lo[:, b, :], bank[0][:], ao_hi[:, b, :].bitcast(F32),
                                  ALU.subtract).then_inc(a_ol, 1)
                for t in range(TB * b, TB * b + TB):
                    dve.wait_ge(a_y, t + 1)
                    dve.tensor_tensor(x[:, t, :], bank[1 + t % 2][:], x[:, t, :], ALU.add)\
                       .then_inc(a_res, 1)
            norm(1, lambda t: dve.wait_ge(a_bod, t + 1))

            def truncate(count, slot):
                dve.wait_ge(f_absd, count)
                dve.tensor_scalar(f_rnd[:, slot, :], f_abs[:, slot, :], 128.0, ROUND, ALU.min, ALU.add)\
                   .then_inc(f_rndd, 1)
                dve.wait_ge(f_rndd, count)
                dve.scalar_tensor_tensor(out=f_off[:, slot, :], in0=f_rnd[:, slot, :], scalar=ROUND,
                                         in1=f_abs[:, slot, :], op0=ALU.subtract, op1=ALU.is_gt)\
                   .then_inc(f_offd, 1)
                dve.wait_ge(f_offd, count)
                dve.wait_ge(f_sgnd, count)
                dve.scalar_tensor_tensor(out=f_val[:, slot, :], in0=f_rnd[:, slot, :], scalar=ROUND,
                                         in1=f_off[:, slot, :], op0=ALU.subtract, op1=ALU.subtract)\
                   .then_inc(f_vald, 1)

            def ffn(n):
                def down_split(i, par):
                    count = 16 * (i // 2 + 1) if isinstance(i, int) else (i - par) * 8 + 16
                    dve.wait_ge(ld_f[n][F_PER * par + 2], count)
                    dve.tensor_scalar(wd_hi[:, i, :], raw[:, F_PER * par + 2, :], 1.0, None, ALU.mult)\
                       .then_inc(wd_h, 1)
                    dve.wait_ge(wd_h, NI * n + i + 1)
                    dve.tensor_tensor(wd_lo[:, i, :], raw[:, F_PER * par + 2, :],
                                      wd_hi[:, i, :].bitcast(F32), ALU.subtract).then_inc(wd_done, 1)

                def quantized(i, b):
                    dve.wait_ge(f_sgd, f_steps * n + NB * i + b + 1)
                    dve.tensor_scalar(inner[:, i, b, :], f_val[:, b, :], 127.0, None, ALU.min)\
                       .then_inc(f_qd, 1)

                def chunk(i, par):
                    for b in range(NB):
                        done = NB * NI * n + NB * i + b
                        dve.wait_ge(f_silu, done + 1)
                        dve.wait_ge(f_up, done + 1)
                        dve.tensor_tensor(f_z[:, b, :], bank[2 * b + 1][:], f_sil[:, b, :], ALU.mult)\
                           .then_inc(f_zd, 1)
                        if b == 0:
                            if not (isinstance(i, int) and i == 0):
                                quantized(i - 1, 1)
                            down_split(i, par)
                        else:
                            quantized(i, 0)
                        truncate(f_steps * n + NB * i + b + 1, b)

                chunk(0, 0)
                chunk(1, 1)
                with dve.Fori(1, NI // 2) as p:
                    for par in range(2):
                        chunk(2 * p + par, par)
                chunk(NI - 1, 0)
                quantized(NI - 1, 1)

                def add(t):
                    dve.wait_ge(f_sgd, f_steps * n + NB * NI + t + 1)
                    dve.scalar_tensor_tensor(out=x[:, t, :], in0=f_val[:, t % 2, :], scalar=127.0,
                                             in1=x[:, t, :], op0=ALU.min, op1=ALU.add).then_inc(f_res, 1)

                for t in range(NT + 1):
                    if t:
                        add(t - 1)
                    if t < NT:
                        truncate(f_steps * n + NB * NI + t + 1, t % 2)

            def run(what, g, b, arg, flags):
                u = NB * g + b
                if what == "kv_out":
                    for half in range(2):
                        ps = bank[half][:].rearrange("p (t n) -> p t n", t=2)
                        ts = slice(2 * half, 2 * half + 2)
                        dve.wait_ge(vh_done, 2 * u + half + 1)
                        if half == 0:
                            need(dve, kt_done, u)
                        dve.tensor_tensor(rk_cos[:, ts, :], ps[:, :, 0:P], tab_k[:, 0, ts, :], ALU.mult)
                        dve.tensor_tensor(rk_sin[:, ts, 0:P // 2], ps[:, :, P // 2:P],
                                          tab_k[:, 1, ts, 0:P // 2], ALU.mult)
                        r = dve.tensor_tensor(rk_sin[:, ts, P // 2:P], ps[:, :, 0:P // 2],
                                              tab_k[:, 1, ts, P // 2:P], ALU.mult)
                    r.then_inc(kv_rot, 1)
                    for half in range(2):
                        ts = slice(2 * half, 2 * half + 2)
                        r = dve.tensor_tensor(v_lo[:, b, ts, :],
                                              bank[half][:].rearrange("p (t n) -> p t n", t=2)[:, :, P:2 * P],
                                              v_hi[:, b, ts, :].bitcast(F32), ALU.subtract)
                    r.then_inc(v_done, 1)
                elif what == "kt":
                    dve.wait_ge(kh_done, u + 1)
                    dve.tensor_tensor(k2_tmp[:], bank[2][:, 0:P], colscale, ALU.mult).then_inc(k2_scaled, 1)
                    dve.tensor_tensor(k1_lo[:, b, 0:P], bank[2][:, 0:P], k1_hi[:, b, 0:P].bitcast(F32),
                                      ALU.subtract)
                    dve.wait_ge(k2_scaled, u + 1)
                    dve.tensor_copy(k2_hi[:, b, 0:P], k2_tmp[:]).then_inc(k2_round, 1)
                    dve.tensor_tensor(k2_lo[:, b, P:SEQ], bank[2][:, P:SEQ],
                                      k2_hi[:, b, P:SEQ].bitcast(F32), ALU.subtract)
                    dve.wait_ge(k2_round, u + 1)
                    dve.tensor_tensor(k2_lo[:, b, 0:P], k2_tmp[:], k2_hi[:, b, 0:P].bitcast(F32),
                                      ALU.subtract).then_inc(k_done, 1)
                elif what == "q" and arg[1] == 1:
                    h = arg[0]
                    ps = bank[Q_BANK[h]]
                    half = P // 2
                    dve.wait_ge(q_done, GH * u + h + 1)
                    need(dve, q_lo, GH * u + h - 1)
                    dve.tensor_tensor(rq_cos[:, h % 2, :], ps[:], tab_q[:, 0, :], ALU.mult)
                    dve.tensor_tensor(rq_sin[0:half, h % 2, :], ps[half:P, :], tab_q[half:P, 1, :], ALU.mult)
                    dve.tensor_tensor(rq_sin[half:P, h % 2, :], ps[0:half, :], tab_q[0:half, 1, :],
                                      ALU.mult).then_inc(q_read, 1)
                elif what == "s":
                    k, h = arg
                    c = 16 * u + GH * k + h
                    w = P * (k + 1)
                    p_out = prob[k % 2][:, h, 0:w]
                    dve.wait_ge(s_done, c + 1)
                    src = bank[3 + h % 2][:, 0:w]
                    if k == 0:
                        dve.tensor_tensor(p_out, src, rowscale, ALU.mult).then_inc(s_scaled, 1)
                        dve.wait_ge(s_scaled, GH * u + h + 1)
                        src = p_out
                    if not (flags[0] and k == 0 and h == 0):
                        sums(c - 1, k if h else (k - 1) % TB, (h - 1) % GH)
                    dve.tensor_tensor_reduce(p_out, src, causal[:, 512 - w:512], -SCALE, -LOWEST,
                                             ALU.add, ALU.min, nmax[:, k, h:h + 1]).then_inc(min_done, 1)
                elif what == "s_end":
                    sums(16 * u + 15, TB - 1, GH - 1)
                elif what == "t":
                    j = PAIRS * u + TRI[arg[0]] + arg[1]
                    par = (TRI[arg[0]] + arg[1]) % 2
                    dve.wait_ge(pth_done, j + 1)
                    dve.tensor_tensor(pt_lo[:, par, :], bank[5 + par][:], pt_hi[:, par, :].bitcast(F32),
                                      ALU.subtract).then_inc(ptl_done, 1)
                elif what == "pv" and arg[0] == arg[1]:
                    dve.wait_ge(oh_done, TB * u + arg[0] + 1)
                    dve.tensor_tensor(o_lo[:].rearrange("p h q -> p (h q)"), bank[7][:],
                                      o_hi[:].rearrange("p h q -> p (h q)").bitcast(F32),
                                      ALU.subtract).then_inc(ol_done, 1)
                elif what == "y":
                    dve.wait_ge(y_done, TB * u + arg + 1)
                    t = TB * b + arg
                    dve.tensor_tensor(x[:, t, :], bank[Y_BANK[arg]][:], x[:, t, :], ALU.add)\
                       .then_inc(y_res, 1)

            def sums(c, k, h):
                dve.wait_ge(exp_done, c + 1)
                dve.reciprocal(rec[:, k, h:h + 1], esum[:, k, h:h + 1]).then_inc(rec_done, 1)

            ffn(0)
            norm(2, lambda t: dve.wait_ge(f_res, t + 1))
            dve.wait_ge(table_in, 48)
            for w in (k1_hi, k1_lo):
                for b in range(NB):
                    dve.memset(w[:, b, P:2 * P].bitcast(F32), 0.0).then_inc(k1_zero, 1)
            walk(dve, run)
            norm(3, lambda t: dve.wait_ge(y_res, TB * (NB * (KVH - 1) + t // TB) + t % TB + 1))
            ffn(1)

        @block.tensor
        def _(pe):
            def product(out_ap, terms, start=True, stop=True):
                n = len(terms)
                for i, (s_hi, s_lo, m_hi, m_lo) in enumerate(terms):
                    pe.matmul(out_ap, s_lo, m_hi, start=start and i == 0, stop=False)
                    pe.matmul(out_ap, s_hi, m_lo, start=False, stop=False)
                    r = pe.matmul(out_ap, s_hi, m_hi, start=False, stop=stop and i == n - 1)
                return r

            def norm(n):
                for t in range(NT):
                    pe.wait_ge(ln_xn, NT * n + t + 1)
                    need(pe, ln_lo, NT * n + t - 1)
                    for c in range(CK):
                        r = pe.transpose(bank[6 + t % 2][:, P * c:P * c + P],
                                         xn_tmp[:, t % 2, P * c:P * c + P], ident[:])
                    r.then_inc(ln_tr, 1)

            pe.wait_ge(ident_ready, 1)
            norm(0)

            for b in range(NB):
                cols = slice(SEQ * b, SEQ * b + SEQ)
                if b == 0:
                    pe.wait_ge(ln_lo, TB)
                    pe.wait_ge(lo_done, 3)
                else:
                    pe.wait_ge(ln_lo, NT)
                for j in range(3):
                    if b:
                        pe.wait_ge(*((a_lo, j + 1) if j < 2 else (a_vt, 1)))
                    product(bank[j][:], [(aw_hi[:, j, c, :], aw_lo[:, j, c, :], xn_hi[:, c, cols],
                                          xn_lo[:, c, cols]) for c in range(CK)]).then_inc(a_proj, 1)
                pe.wait_ge(a_vt, b + 1)
                need(pe, a_v, b)
                for kt in range(TB):
                    r = pe.transpose(bank[3][:, P * kt:P * kt + P], a_vT[:, b, P * kt:P * kt + P], ident[:])
                r.then_inc(a_vtr, 1)
            for t in range(NT):
                b, qb = divmod(t, TB)
                pe.wait_ge(a_lo, 2 * b + 2)
                need(pe, a_min, t - 1)
                q = slice(P * qb, P * qb + P)
                product(bank[4 + t % 2][:], [(aqk_hi[:, b, 0, q], aqk_lo[:, b, 0, q],
                                              aqk_hi[:, b, 1, :], aqk_lo[:, b, 1, :])]).then_inc(a_s, 1)
            for b in range(NB):
                pe.wait_ge(a_norm, TB * b + TB)
                pe.wait_ge(a_v, b + 1)

                def turn(kt):
                    need(pe, a_ptl, TB * b + kt - 1)
                    for qb in range(TB):
                        r = pe.transpose(bank[6 + kt % 2][:, P * qb:P * qb + P],
                                         a_p[:, b, qb, P * kt:P * kt + P], ident[:])
                    r.then_inc(a_pt, 1)

                turn(0)
                for kt in range(TB):
                    if kt + 1 < TB:
                        turn(kt + 1)
                    pe.wait_ge(a_ptl, TB * b + kt + 1)
                    if kt == 0:
                        need(pe, a_ol, b)
                    r = product(bank[0][:], [(av_hi[:, b, kt, :], av_lo[:, b, kt, :], apt_hi[:, kt % 2, :],
                                              apt_lo[:, kt % 2, :])], start=kt == 0, stop=kt == TB - 1)
                r.then_inc(a_pv, 1)
                pe.wait_ge(a_ol, b + 1)
                pe.wait_ge(lo_done, A_PIECES)
                for qb in range(TB):
                    t = TB * b + qb
                    need(pe, a_res, t - 1)
                    q = slice(P * qb, P * qb + P)
                    product(bank[1 + t % 2][:], [(ao_hi[:, b, q], ao_lo[:, b, q], a_part(aw_hi, 3),
                                                  a_part(aw_lo, 3))]).then_inc(a_y, 1)

            def ffn(n):
                def chunk(i, par):
                    for b in range(NB):
                        cols = slice(SEQ * b, SEQ * b + SEQ)
                        done = NB * NI * n + NB * i + b
                        if b == 0:
                            pe.wait_ge(lo_done, lo_f[n] + 2 * i + 2)
                        need(pe, f_zd, done - 1)
                        for j in range(2):
                            product(bank[2 * b + j][:],
                                    [(wgu_hi[:, par, j, c, :], wgu_lo[:, par, j, c, :], xn_hi[:, c, cols],
                                      xn_lo[:, c, cols]) for c in range(CK)])\
                                .then_inc((f_gate, f_up)[j], 1)

                norm(1 + 2 * n)
                pe.wait_ge(ln_lo, NT * (2 + 2 * n))
                chunk(0, 0)
                chunk(1, 1)
                with pe.Fori(1, NI // 2) as p:
                    for par in range(2):
                        chunk(2 * p + par, par)
                chunk(NI - 1, 0)
                pe.wait_ge(wd_done, NI * (n + 1))
                for t in range(NT):
                    b, q = t // TB, slice(P * (t % TB), P * (t % TB) + P)
                    pe.wait_ge(f_qd, NB * NI * (n + 1) - 1 + b)
                    if t > 1:
                        pe.wait_ge(f_sgnd, f_steps * n + NB * NI + t - 1)
                    for i in range(NI):
                        pe.matmul(bank[4 + t % 2][:], inner[:, i, b, q], wd_lo[:, i, :], start=i == 0,
                                  stop=False)
                        r = pe.matmul(bank[4 + t % 2][:], inner[:, i, b, q], wd_hi[:, i, :], start=False,
                                      stop=i == NI - 1)
                    r.then_inc(f_y, 1)

            def run(what, g, b, arg, flags):
                u = NB * g + b
                first, last = flags
                start_up = isinstance(u, int) and u == 0
                if what == "kv":
                    t = arg
                    if t == 0:
                        pe.wait_ge(lo_done, lo_b + B_PER * g + 2)
                    if t in (0, 2) and not (isinstance(u, int) and u < 2):
                        pe.wait_ge(y_res, TB * (u - 2) + t // 2 + 1)
                    tok = slice(SEQ * b + P * t, SEQ * b + P * t + P)
                    r = product(bank[t // 2][:, 2 * P * (t % 2):2 * P * (t % 2) + 2 * P],
                                [(xn_hi[:, c, tok], xn_lo[:, c, tok], wkv_hi[:, c, :], wkv_lo[:, c, :])
                                 for c in range(CK)])
                    if t % 2:
                        r.then_inc(kv_done, 1)
                elif what == "q":
                    h, half = arg
                    if half == 0:
                        pe.wait_ge(lo_done, lo_b + B_PER * g + 3 + h)
                        if h < 2:
                            pe.wait_ge(v_done, u + 1)
                        elif h == 2:
                            pe.wait_ge(k_done, u + 1)
                        else:
                            pe.wait_ge(q_read, GH * u + 3)
                    cols = slice(SEQ * b, SEQ * b + SEQ)
                    r = product(bank[Q_BANK[h]][:],
                                [(wq_hi[:, h, c, :], wq_lo[:, h, c, :], xn_hi[:, c, cols], xn_lo[:, c, cols])
                                 for c in (2 * half, 2 * half + 1)], start=half == 0, stop=half == 1)
                    if half:
                        r.then_inc(q_done, 1)
                elif what == "kt":
                    pe.wait_ge(kv_rope, u + 1)
                    if not (isinstance(u, int) and u < 2):
                        pe.wait_ge(y_res, TB * (u - 1))
                    for t in range(TB):
                        r = pe.transpose(bank[2][:, P * t:P * t + P], rk_cos[:, t, :], ident[:])
                    r.then_inc(kt_done, 1)
                elif what == "s":
                    k, h = arg
                    c = 16 * u + GH * k + h
                    if k == 0 and h == 0:
                        pe.wait_ge(k_done, u + 1)
                    if k == 0:
                        pe.wait_ge(q_lo, GH * u + h + 1)
                    need(pe, min_done, c - 1)
                    q = slice(P * k, P * k + P)
                    w = max(2, k + 1) * P
                    keys = (k1_hi[:, b, :], k1_lo[:, b, :]) if k == 0 else (k2_hi[:, b, 0:w], k2_lo[:, b, 0:w])
                    product(bank[3 + h % 2][:, 0:w], [(qT_hi[:, b, h, q], qT_lo[:, b, h, q], *keys)])\
                        .then_inc(s_done, 1)
                elif what == "t":
                    k, kt = arg
                    if kt == 0:
                        pe.wait_ge(norm_done, 16 * u + GH * k + GH)
                    par = (TRI[k] + kt) % 2
                    need(pe, ptl_done, PAIRS * u + TRI[k] + kt - 1)
                    for h in range(GH):
                        r = pe.transpose(bank[5 + par][:, P * h:P * h + P],
                                         prob[k % 2][:, h, P * kt:P * kt + P], ident[:])
                    r.then_inc(pt_done, 1)
                elif what == "pv":
                    k, kt = arg
                    par = (TRI[k] + kt) % 2
                    pe.wait_ge(ptl_done, PAIRS * u + TRI[k] + kt + 1)
                    if kt == 0:
                        need(pe, ol_done, TB * u + k)
                    r = product(bank[7][:], [(v_hi[:, b, kt, :], v_lo[:, b, kt, :], pt_hi[:, par, :],
                                              pt_lo[:, par, :])], start=kt == 0, stop=kt == k)
                    if kt == k:
                        r.then_inc(o_done, 1)
                elif what == "y":
                    k = arg
                    pe.wait_ge(ol_done, TB * u + k + 1)
                    if k == 0:
                        pe.wait_ge(lo_done, lo_b + B_PER * g + B_PER)
                    if last and k < 2:
                        pe.wait_ge(y_res, TB * u)
                    elif k == 0:
                        pe.wait_ge(q_read, GH * (u + 1) + 1)
                    elif k == 1:
                        pe.wait_ge(q_read, GH * (u + 1) + 2)
                    elif k == 2:
                        if not last:
                            pe.wait_ge(q_read, GH * (u + 1) + 4)
                    else:
                        pe.wait_ge(y_res, TB * u + 3)
                    product(bank[Y_BANK[k]][:], [(o_hi[:, h, :], o_lo[:, h, :], wo_hi[:, h, :],
                                                  wo_lo[:, h, :]) for h in range(GH)]).then_inc(y_done, 1)

            ffn(0)
            norm(2)
            pe.wait_ge(ln_lo, 3 * NT)
            pe.wait_ge(k1_zero, 2 * NB)
            walk(pe, run)
            ffn(1)


Q_BANK = [0, 1, 2, 2]
Y_BANK = [0, 1, 2, 2]


def tables():
    inv = (np.float32(1.0) / np.float32(10000.0) ** (np.arange(0, P, 2, dtype=np.float32) / np.float32(P)))
    ang = np.arange(SEQ, dtype=np.float32)[:, None] * inv[None, :].astype(np.float32)
    emb = np.concatenate([ang, ang], axis=1)
    cos, sin = np.cos(emb).astype(np.float32), np.sin(emb).astype(np.float32)
    signed = np.concatenate([-sin[:, :P // 2], sin[:, P // 2:]], axis=1)
    swapped = np.concatenate([signed[:, P // 2:], signed[:, :P // 2]], axis=1)
    rope_q = np.ascontiguousarray(np.stack([cos.T, swapped.T], axis=1))
    rope_k = np.stack([cos, signed]).reshape(2, TB, P, P).transpose(2, 0, 1, 3)
    q, k = np.arange(P)[:, None], np.arange(P)[None, :]
    causal = np.zeros((P, 4 * P), np.float32)
    causal[:, 3 * P:] = np.where(q >= k, 0.0, LOWEST)
    keys = np.where(k < SYS, 0.5, np.where(k < BOOST, 1.5, 1.0))
    rows = np.where(q >= BOOST, keys, 1.0)
    masks = np.concatenate([causal, rows, np.broadcast_to(keys, (P, P))], axis=1)
    return rope_q, np.ascontiguousarray(rope_k), np.ascontiguousarray(masks.astype(np.float32))


def kernel(**inputs):
    import concourse.bacc as bacc
    from concourse.bass_utils import run_bass_kernel_spmd

    a = {k.removeprefix("L0_"): np.asarray(v) for k, v in inputs.items()}
    pad = NI * P - INTER

    def columns(w, n):
        return w.reshape(CK, P, n, P).transpose(2, 1, 0, 3).reshape(n, P, CK * P)

    gate = columns(np.pad(a["ffn_w_gate"], ((0, pad), (0, 0))).T, NI)
    up = columns(np.pad(a["ffn_w_up"], ((0, pad), (0, 0))).T, NI)
    down = np.pad(a["ffn_w_down"], ((0, 0), (0, pad))).T.reshape(NI, P, C)
    ffn = np.stack([gate, up, down], axis=1).reshape(NI * F_PER, P, C)
    kv = np.stack([a["attn_b_wk"].reshape(KVH, P, C), a["attn_b_wv"].reshape(KVH, P, C)], axis=1)
    kv = kv.reshape(KVH, 2, P, 2, 2, P).transpose(0, 3, 5, 4, 1, 2).reshape(KVH, 2, P, C)
    wq = columns(a["attn_b_wq"].T, HEADS).reshape(KVH, GH, P, C)
    wo = a["attn_b_wo"].T.reshape(KVH, GH, P, C)
    att = np.concatenate([kv, wq, wo], axis=1).reshape(KVH * B_PER, P, C)
    weights = np.concatenate([columns(a["attn_a_Wqkv"], 3), a["attn_a_Wo"][None], ffn, att])
    rope_q, rope_k, masks = tables()
    arrays = {
        "x": np.ascontiguousarray(a["attn_a_x"]),
        "weights": np.ascontiguousarray(weights),
        "bqkv": np.ascontiguousarray(a["attn_a_bqkv"].reshape(3, P).T),
        "bo": np.ascontiguousarray(np.broadcast_to(a["attn_a_bo"], (P, C))),
        "rope_q": rope_q, "rope_k": rope_k, "masks": masks,
    }
    nc = bacc.Bacc("TRN2", target_bir_lowering=False, num_devices=1)
    args = [nc.dram_tensor(n, v.shape, mybir.dt.from_np(v.dtype), kind="ExternalInput").ap()
            for n, v in arrays.items()]
    out = nc.dram_tensor("out", a["attn_a_x"].shape, F32, kind="ExternalOutput").ap()
    build(nc, *args, out)
    return run_bass_kernel_spmd(nc, [arrays], core_ids=[0]).results[0]["out"]
```

```python
from contextlib import ExitStack

import numpy as np
import concourse.bass as bass
from concourse import mybir

F32 = mybir.dt.float32
F32R = mybir.dt.float32r
ALU = mybir.AluOpType
ACT = mybir.ActivationFunctionType

P = 128
NB = 2
SEQ = 512
TB = SEQ // P
NT = NB * TB
C = 512
CK = C // P
INTER = 1376
NI = -(-INTER // P)
HEADS, KVH = 32, 8
GH = HEADS // KVH
SYS, IMG = 35, 72
BOOST = SYS + IMG
SCALE = float(1.0 / np.sqrt(np.float32(P)))
EPS = 1e-5
LOWEST = float(np.finfo(np.float32).min)
ROUND = float(3 << 22)
TRI = [0, 1, 3, 6]
PAIRS = 10

A_PIECES = 4
F_PER = 3
B_PER = 10
F_BASE = A_PIECES
B_BASE = F_BASE + F_PER * NI
RAW = 6
B_RAW = 5


def need(eng, sem, count):
    if not (isinstance(count, int) and count <= 0):
        eng.wait_ge(sem, count)


def build(nc, x_in, weights, bqkv, bo, rope_q, rope_k, masks, out):
    with ExitStack() as ctx:
        place = [nc.sbuf_base]

        def sb(name, shape, dt=F32):
            size = int(np.prod(shape[1:])) * 4
            t = nc.alloc_sbuf_tensor_at(name, shape, dt, offset=place[0])
            place[0] += -(-size // 32) * 32
            return t

        def sem(name):
            return ctx.enter_context(nc.semaphore(name))

        place[0] = -(-place[0] // 32) * 32
        x = sb("x", [P, NT, C])
        xn_hi = sb("xn_hi", [P, CK, NT * P], F32R)
        xn_lo = sb("xn_lo", [P, CK, NT * P], F32R)
        ident = sb("ident", [P, P])
        raw = sb("raw", [P, RAW, C])
        stats = sb("stats", [P, NT, 6])
        mv = sb("mv", [P, NT, 2])
        vare = sb("vare", [P, NT, 1])
        rstd = sb("rstd", [P, NT, 1])
        mhalf = sb("mhalf", [P, TB, 1])
        xn_tmp = sb("xn_tmp", [P, 2, C])
        tab_q = sb("tab_q", [P, 2, SEQ])
        tab_k = sb("tab_k", [P, 2, TB, P])
        tab_m = sb("tab_m", [P, 512 + 2 * P])
        start = place[0]

        wgu_hi = sb("wgu_hi", [P, 2, 2, CK, P], F32R)
        wgu_lo = sb("wgu_lo", [P, 2, 2, CK, P], F32R)
        after_gu = place[0]
        wd_hi = sb("wd_hi", [P, NI, C], F32R)
        wd_lo = sb("wd_lo", [P, NI, C], F32R)
        inner = sb("inner", [P, NI, NB, SEQ], F32R)
        after_inner = place[0]
        f_sil = sb("f_sil", [P, 2, 512])
        f_z = sb("f_z", [P, 2, 512])
        f_abs = sb("f_abs", [P, 2, 512])
        f_sgn = sb("f_sgn", [P, 2, 512])
        f_rnd = sb("f_rnd", [P, 2, 512])
        f_off = sb("f_off", [P, 2, 512])
        f_val = sb("f_val", [P, 2, 512])
        top = place[0]

        place[0] = after_gu
        aw_hi = sb("aw_hi", [P, 4, CK, P], F32R)
        aw_lo = sb("aw_lo", [P, 4, CK, P], F32R)
        a_bias = sb("a_bias", [P, 3])
        a_bo = sb("a_bo", [P, C])
        aqk_hi = sb("aqk_hi", [P, NB, 2, SEQ], F32R)
        aqk_lo = sb("aqk_lo", [P, NB, 2, SEQ], F32R)
        a_vT = sb("a_vT", [P, NB, SEQ])
        av_hi = sb("av_hi", [P, NB, TB, P], F32R)
        av_lo = sb("av_lo", [P, NB, TB, P], F32R)
        a_p = sb("a_p", [P, NB, TB, SEQ])
        a_nmax = sb("a_nmax", [P, NT])
        a_sum = sb("a_sum", [P, NT])
        a_rec = sb("a_rec", [P, NT])
        apt_hi = sb("apt_hi", [P, 2, SEQ], F32R)
        apt_lo = sb("apt_lo", [P, 2, SEQ], F32R)
        ao_hi = sb("ao_hi", [P, NB, SEQ], F32R)
        ao_lo = sb("ao_lo", [P, NB, SEQ], F32R)
        assert place[0] <= top

        place[0] = start
        wq_hi = sb("wq_hi", [P, GH, CK, P], F32R)
        wq_lo = sb("wq_lo", [P, GH, CK, P], F32R)
        assert place[0] == after_gu
        wo_hi = sb("wo_hi", [P, GH, C], F32R)
        wo_lo = sb("wo_lo", [P, GH, C], F32R)
        qT_hi = sb("qT_hi", [P, NB, GH, SEQ], F32R)
        qT_lo = sb("qT_lo", [P, NB, GH, SEQ], F32R)
        k1_hi = sb("k1_hi", [P, NB, 2 * P], F32R)
        k1_lo = sb("k1_lo", [P, NB, 2 * P], F32R)
        k2_hi = sb("k2_hi", [P, NB, SEQ], F32R)
        k2_lo = sb("k2_lo", [P, NB, SEQ], F32R)
        pt_hi = sb("pt_hi", [P, 2, 512], F32R)
        pt_lo = sb("pt_lo", [P, 2, 512], F32R)
        o_hi = sb("o_hi", [P, 2, GH, P], F32R)
        o_lo = sb("o_lo", [P, 2, GH, P], F32R)
        v_hi = sb("v_hi", [P, NB, TB, P], F32R)
        prob0 = sb("prob0", [P, GH, 3 * P])
        k2_tmp = sb("k2_tmp", [P, P])
        nmax = sb("nmax", [P, TB, GH])
        esum = sb("esum", [P, TB, GH])
        rec = sb("rec", [P, TB, GH])
        assert place[0] <= after_inner
        place[0] = after_inner
        wkv_hi = sb("wkv_hi", [P, CK, 2 * P], F32R)
        wkv_lo = sb("wkv_lo", [P, CK, 2 * P], F32R)
        prob1 = sb("prob1", [P, GH, 4 * P])
        rq_cos = sb("rq_cos", [P, 2, 512])
        rq_sin = sb("rq_sin", [P, 2, 512])
        v_lo = sb("v_lo", [P, NB, TB, P], F32R)
        rk_cos = xn_tmp[:, 0, :].rearrange("p (t d) -> p t d", t=TB)
        rk_sin = xn_tmp[:, 1, :].rearrange("p (t d) -> p t d", t=TB)
        assert max(place[0], top) <= nc.sbuf_usable_end
        causal = tab_m[:, 0:512]
        rowscale = tab_m[:, 512:640]
        colscale = tab_m[:, 640:768]
        prob = [prob0, prob1]

        bank = [ctx.enter_context(nc.psum_tensor(f"bank{i}", [P, 512], F32)) for i in range(8)]

        x_in_sem = [sem(f"x_in_{t}") for t in range(NT)]
        ident_set = sem("ident_set")
        ident_ready = sem("ident_ready")
        small_in = sem("small_in")
        table_in = sem("table_in")
        ld_a = [sem(f"ld_a{j}") for j in range(A_PIECES)]
        ld_f = [[sem(f"ld_f{n}_{j}") for j in range(RAW)] for n in range(2)]
        ld_b = [sem(f"ld_b{j}") for j in range(B_RAW)]
        hi_done = sem("hi_done")
        lo_done = sem("lo_done")
        wd_h = sem("wd_h")
        wd_done = sem("wd_done")
        stored = sem("stored")
        ln_stat, ln_aggr, ln_eps, ln_rstd = sem("ln_stat"), sem("ln_aggr"), sem("ln_eps"), sem("ln_rstd")
        ln_xn, ln_tr, ln_hi, ln_lo = sem("ln_xn"), sem("ln_tr"), sem("ln_hi"), sem("ln_lo")
        a_proj, a_qk, a_lo, a_vt, a_vtr, a_vh, a_v = (sem(n) for n in (
            "a_proj", "a_qk", "a_lo", "a_vt", "a_vtr", "a_vh", "a_v"))
        a_s, a_min, a_exp, a_recd, a_norm = (sem(n) for n in ("a_s", "a_min", "a_exp", "a_recd", "a_norm"))
        a_pt, a_pth, a_ptl, a_pv, a_oh, a_ol, a_y, a_res, a_bod = (sem(n) for n in (
            "a_pt", "a_pth", "a_ptl", "a_pv", "a_oh", "a_ol", "a_y", "a_res", "a_bod"))
        f_gate, f_up, f_silu, f_zd, f_absd, f_sgnd, f_rndd, f_offd, f_vald, f_sgd, f_qd = (
            sem(n) for n in ("f_gate", "f_up", "f_silu", "f_zd", "f_absd", "f_sgnd", "f_rndd",
                             "f_offd", "f_vald", "f_sgd", "f_qd"))
        f_y, f_res = sem("f_y"), sem("f_res")
        kv_done, kv_rot, kv_rope, kt_done, kh_done, k2_scaled, k2_round, k_done, vh_done, v_done = (
            sem(n) for n in ("kv_done", "kv_rot", "kv_rope", "kt_done", "kh_done", "k2_scaled",
                             "k2_round", "k_done", "vh_done", "v_done"))
        k1_zero = sem("k1_zero")
        q_done, q_read, q_sum, q_hi, q_lo = (
            sem(n) for n in ("q_done", "q_read", "q_sum", "q_hi", "q_lo"))
        s_done, s_scaled, min_done, exp_done, rec_done, norm_done = (
            sem(n) for n in ("s_done", "s_scaled", "min_done", "exp_done", "rec_done", "norm_done"))
        pv_done = sem("pv_done")
        pt_done, pth_done, ptl_done, oh_done, ol_done, y_done, y_res = (
            sem(n) for n in ("pt_done", "pth_done", "ptl_done", "oh_done", "ol_done",
                             "y_done", "y_res"))

        lo_f = [A_PIECES, A_PIECES + 2 * NI + B_PER * KVH]
        lo_b = A_PIECES + 2 * NI

        def consumed(s):
            if s < A_PIECES:
                return s, (lo_done, s + 1)
            n = 0 if s < B_BASE else 1
            if n and s < B_BASE + B_PER * KVH:
                g, j = divmod(s - B_BASE, B_PER)
                return j % B_RAW, (lo_done, lo_b + B_PER * g + j + 1)
            i, j = divmod(s - (F_BASE if not n else B_BASE + B_PER * KVH), F_PER)
            done = (wd_done, NI * n + i + 1) if j == 2 else (lo_done, lo_f[n] + 2 * i + j + 1)
            return F_PER * (i % 2) + j, done

        def before(s):
            slot = consumed(s)[0]
            for r in range(s - 1, -1, -1):
                if consumed(r)[0] == slot:
                    return consumed(r)[1]
            return None

        block = ctx.enter_context(nc.Block())

        @block.sync
        def _(sp):
            def load(s, piece, slot, sem_):
                w = before(s)
                if w:
                    sp.wait_ge(*w)
                sp.dma_start(raw[:, slot, :], weights[piece]).then_inc(sem_, 16)

            for s in range(A_PIECES):
                load(s, s, s, ld_a[s])

            def ffn(n):
                base = F_BASE if n == 0 else B_BASE + B_PER * KVH

                def chunk(i):
                    for j in range(F_PER):
                        load(base + F_PER * i + j, F_BASE + F_PER * i + j, F_PER * (i % 2) + j,
                             ld_f[n][F_PER * (i % 2) + j])

                chunk(0)
                chunk(1)
                with sp.Fori(1, NI // 2) as p:
                    for par in range(2):
                        i = 2 * p + par
                        for j in range(F_PER):
                            if j == 2:
                                sp.wait_ge(wd_done, NI * n + i - 1)
                            else:
                                sp.wait_ge(lo_done, lo_f[n] + 2 * i - 4 + j + 1)
                            sp.dma_start(raw[:, F_PER * par + j, :], weights[F_BASE + F_PER * i + j])\
                              .then_inc(ld_f[n][F_PER * par + j], 16)
                chunk(NI - 1)

            ffn(0)
            for j in range(B_PER):
                load(B_BASE + j, B_BASE + j, j % B_RAW, ld_b[j % B_RAW])
            with sp.Fori(1, KVH) as g:
                for j in range(B_PER):
                    sp.wait_ge(lo_done, lo_b + B_PER * g + j - B_RAW + 1)
                    sp.dma_start(raw[:, j % B_RAW, :], weights[B_BASE + B_PER * g + j])\
                      .then_inc(ld_b[j % B_RAW], 16)
            ffn(1)

            out_t = out.rearrange("b (t p) c -> p (b t) c", p=P)
            for t in range(NT):
                sp.wait_ge(f_res, NT + t + 1)
                sp.dma_start(out_t[:, t, :], x[:, t, :]).then_inc(stored, 16)
            sp.wait_ge(stored, 16 * NT)


        def unit_order(b, first, last, group_first, group_last, early=()):
            fill = {
                (0, 0): [("q_out", 0, 3), ("kv", 1, 0)],
                (0, 1): [("kv", 1, 1)],
                (0, 2): [("y", -1, 2)],
                (0, 3): [("kv", 1, 2), ("kv_out", 1, 0)],
                (1, 0): [("kv", 1, 3)],
                (1, 1): [("q", 1, (0, 0))],
                (1, 2): [("q", 1, (0, 1)), ("kv_out", 1, 1)],
                (1, 3): [("y", -1, 3)],
                (2, 0): [("q", 1, (1, 0)), ("kt", 1, 0), ("q_out", 1, 0)],
                (2, 1): [("q", 1, (1, 1))],
                (2, 2): [("q", 1, (2, 0))],
                (2, 3): [("q", 1, (2, 1))],
                (3, 0): [("y", 0, 0), ("q_out", 1, 1)],
                (3, 1): [("y", 0, 1)],
                (3, 2): [("q", 1, (3, 0)), ("q_out", 1, 2)],
                (3, 3): [("q", 1, (3, 1))],
            }
            if b == 0:
                if not group_first:
                    for i, at in enumerate(((1, 3), (2, 0), (2, 1), (2, 2))):
                        fill[at].append(("w", 0, 6 + i))
                if not group_last:
                    fill[(2, 3)].append(("w", 2, 0))
                    fill[(3, 1)].append(("w", 2, 1))
            elif not group_last:
                for i in range(4):
                    fill[(0, i)].append(("w", 1, 2 + i))
            turn_at, use_at = {}, {}
            for back in (-1, 0):
                for tile in range(TB):
                    for kt in range(tile + 1):
                        at = 4 * TB * back + GH * (tile + 1) + kt + 1
                        for when, table in ((at, turn_at), (at + 1, use_at)):
                            if 0 <= when < 4 * TB:
                                table[divmod(when, GH)] = (back, (tile, kt))
            if last:
                fill[(0, 0)].append(("gu", 0, 0))
                for at, stages in (((0, 1), "a0"), ((0, 2), "a1 b0"), ((1, 0), "t0 b1 a2"),
                                   ((1, 1), "c0"), ((1, 2), "t1 b2"), ((1, 3), "c1"),
                                   ((2, 0), "t2 a3"), ((2, 1), "c2 b3"), ((2, 3), "t3"),
                                   ((3, 0), "c3"), ((3, 1), "a4"), ((3, 2), "b4"),
                                   ((3, 3), "a5")):
                    fill[at] += [("ln", 0, (w[0], 3, int(w[1]))) for w in stages.split()]
            order = []
            for k in range(TB):
                for h in range(GH):
                    order.append(("s", 0, (k, h)))
                    if (k, h) in early:
                        order.append(("t", *turn_at[(k, h)]))
                    order += fill[(k, h)]
                    if (k, h) in use_at:
                        order.append(("pv", *use_at[(k, h)]))
                    if (k, h) in turn_at and (k, h) not in early:
                        order.append(("t", *turn_at[(k, h)]))
            keep = []
            for what, d, arg in order:
                if d == -1 and first:
                    continue
                if d == 1 and last and what != "w":
                    continue
                keep.append((what, d, arg))
            return keep

        FIRST_UNIT = [("kv", 0, 0), ("kv", 0, 1), ("ln", 0, ("tail", 2, 5)), ("kv", 0, 2), ("kv", 0, 3),
                      ("ln", 0, ("tail", 2, 6)), ("q", 0, (0, 0)), ("ln", 0, ("tail", 2, 7)),
                      ("kv_out", 0, 0), ("kv_out", 0, 1), ("q", 0, (0, 1)), ("q", 0, (1, 0)), ("kt", 0, 0),
                      ("q", 0, (1, 1)), ("q_out", 0, 0), ("q", 0, (2, 0)),
                      ("q", 0, (2, 1)), ("q_out", 0, 1), ("q", 0, (3, 0)), ("q", 0, (3, 1)),
                      ("q_out", 0, 2)]
        LAST_TURN = [("s_end", 0, 0), ("pv", 0, (2, 2)), ("t", 0, (3, 0)), ("ln", 0, ("b", 3, 5)),
                     ("ln", 0, ("t", 3, 4)), ("t", 0, (3, 1)), ("y", 0, 2), ("ln", 0, ("c", 3, 4)),
                     ("pv", 0, (3, 0)), ("t", 0, (3, 2)), ("ln", 0, ("t", 3, 5)), ("pv", 0, (3, 1)),
                     ("ln", 0, ("a", 3, 6)), ("t", 0, (3, 3)), ("ln", 0, ("c", 3, 5)), ("pv", 0, (3, 2)),
                     ("ln", 0, ("b", 3, 6)), ("pv", 0, (3, 3)), ("ln", 0, ("t", 3, 6)), ("y", 0, 3),
                     ("ln", 0, ("c", 3, 6))]

        def walk(eng, run, early=()):
            for what, _, arg in FIRST_UNIT:
                run(what, 0, 0, arg, (True, False))

            def group(g, group_first=False, group_last=False):
                for b in range(NB):
                    first, last = group_first and b == 0, group_last and b == 1
                    for what, d, arg in unit_order(b, first, last, group_first, group_last, early):
                        if what == "w":
                            run(what, g + (1 if arg < 6 else 0), 0, arg, (first, last))
                        else:
                            run(what, g + (b + d) // NB, (b + d) % NB, arg, (first, last))

            group(0, group_first=True)
            with eng.Fori(1, KVH - 1) as g:
                group(g)
            group(KVH - 1, group_last=True)
            for what, _, arg in LAST_TURN:
                run(what, KVH - 1, NB - 1, arg, (False, True))

        def w_parts(j):
            if j < 2:
                return tuple(w[:, 2 * j:2 * j + 2, :].rearrange("p c d -> p (c d)") for w in (wkv_hi, wkv_lo))
            if j < 6:
                return tuple(w[:, j - 2].rearrange("p c d -> p (c d)") for w in (wq_hi, wq_lo))
            return wo_hi[:, j - 6, :], wo_lo[:, j - 6, :]

        def gu_part(w, par, j):
            return w[:, par, j].rearrange("p c d -> p (c d)")

        def a_part(w, j):
            return w[:, j].rearrange("p c d -> p (c d)")

        def ln_bank(n, t):
            if n == 3:
                return bank[1] if t < TB else bank[3 + t % 2]
            return bank[6 + t % 2]

        def q_bank(u, h):
            return 3 + h if isinstance(u, int) and u == 0 else Q_BANK[h]

        def a_y_bank(t):
            return bank[[1, 2, 3, 0, 4, 5, 3, 2][t]]

        f_steps = NB * NI + NT

        @block.gpsimd
        def _(pool):
            pool.memset(ident[:], 0.0).then_inc(ident_set, 1)
            pool.memset(mhalf[:], -0.5).then_inc(ident_set, 1)
            pool.wait_ge(ident_set, 2)
            pool.affine_select(out=ident[:], in_=ident[:], compare_op=ALU.not_equal, fill=1.0, base=0,
                               pattern=[[-1, P]], channel_multiplier=1).then_inc(ident_ready, 1)

            def split_lo(count, slot, hi, lo):
                pool.wait_ge(hi_done, count)
                pool.tensor_tensor(lo, raw[:, slot, :], hi.bitcast(F32), ALU.subtract)\
                    .then_inc(lo_done, 1)

            def norm(n, tiles):
                for t in tiles:
                    pool.wait_ge(ln_eps, NT * n + t + 1)
                    pool.tensor_tensor(rstd[:, t, :], vare[:, t, :], mhalf[:, 0, :], ALU.pow)\
                        .then_inc(ln_rstd, 1)

            def norm_batch(n, t0):
                pool.wait_ge(ln_eps, NT * n + t0 + TB)
                pool.tensor_tensor(rstd[:, t0:t0 + TB, :], vare[:, t0:t0 + TB, :], mhalf[:], ALU.pow)\
                    .then_inc(ln_rstd, TB)

            def signs(count, slot):
                pool.wait_ge(f_vald, count)
                pool.tensor_tensor(f_val[:, slot, :], f_val[:, slot, :], f_sgn[:, slot, :], ALU.mult)\
                    .then_inc(f_sgd, 1)

            def gu_lo(n, i, par):
                for j in range(2):
                    split_lo(lo_f[n] + 2 * i + j + 1, F_PER * par + j,
                             gu_part(wgu_hi, par, j), gu_part(wgu_lo, par, j))

            def ffn(n):
                def chunk(i, par, last=False):
                    if not last:
                        gu_lo(n, i + 1, 1 - par)
                    for b in range(NB):
                        signs(f_steps * n + NB * i + b + 1, b)

                chunk(0, 0)
                chunk(1, 1)
                with pool.Fori(1, NI // 2) as p:
                    for par in range(2):
                        chunk(2 * p + par, par)
                chunk(NI - 1, 0, last=True)
                if n == 0:
                    for j in range(6):
                        run("w", 0, 0, j, None)
                for t in range(NT):
                    signs(f_steps * n + NB * NI + t + 1, t % 2)
                    if n == 0 and t:
                        norm(2, [t - 1])

            def run(what, g, b, arg, flags):
                u = NB * g + b
                if what == "ln" and arg[0] == "a":
                    norm(arg[1], [arg[2]])
                elif what == "gu":
                    gu_lo(1, 0, 0)
                elif what == "w":
                    split_lo(lo_b + B_PER * g + arg + 1, arg % B_RAW, *w_parts(arg))
                elif what == "kv_out" and arg == 1:
                    pool.wait_ge(kv_rot, 2 * u + 2)
                    pool.tensor_tensor(rk_cos, rk_cos, rk_sin, ALU.add).then_inc(kv_rope, 1)
                elif what == "q" and arg[1] == 1:
                    h = arg[0]
                    pool.wait_ge(q_read, GH * u + h + 1)
                    pool.tensor_tensor(rq_cos[:, h % 2, :], rq_cos[:, h % 2, :], rq_sin[:, h % 2, :],
                                       ALU.add).then_inc(q_sum, 1)
                elif what == "q_out" and not (isinstance(u, int) and u == 0):
                    h = arg
                    pool.wait_ge(q_hi, GH * u + h + 1)
                    pool.tensor_tensor(qT_lo[:, b, h, :], rq_cos[:, h % 2, :],
                                       qT_hi[:, b, h, :].bitcast(F32), ALU.subtract).then_inc(q_lo, 1)

            norm(0, range(TB))
            for j in range(A_PIECES):
                if j == 3:
                    norm_batch(0, TB)
                split_lo(j + 1, j, a_part(aw_hi, j), a_part(aw_lo, j))
            pool.wait_ge(small_in, 32)
            for t in range(NT):
                pool.wait_ge(ln_xn, t + 1)
                pool.tensor_tensor(x[:, t, :], x[:, t, :], a_bo[:], ALU.add).then_inc(a_bod, 1)
            gu_lo(0, 0, 0)
            for b in range(NB):
                norm_batch(1, TB * b)
            ffn(0)
            norm(2, [NT - 1])
            for j in range(6, B_PER):
                run("w", 0, 0, j, None)
            walk(pool, run)
            norm(3, [NT - 1])
            ffn(1)

        @block.scalar
        def _(act):
            x_t = x_in.rearrange("b (t p) c -> p (b t) c", p=P)
            for t in range(NT):
                act.dma_start(x[:, t, :], x_t[:, t, :]).then_inc(x_in_sem[t], 16)
            act.dma_start(a_bias[:], bqkv).then_inc(small_in, 16)
            act.dma_start(a_bo[:], bo).then_inc(small_in, 16)
            act.dma_start(tab_q[:], rope_q).then_inc(table_in, 16)
            act.dma_start(tab_k[:], rope_k).then_inc(table_in, 16)
            act.dma_start(tab_m[:], masks).then_inc(table_in, 16)

            def split_hi(slot, ready, count, hi):
                act.wait_ge(ready, count)
                act.activation(hi, raw[:, slot, :], ACT.Copy).then_inc(hi_done, 1)

            def norm(n, tiles):
                for t in tiles:
                    act.wait_ge(ln_tr, NT * n + t + 1)
                    act.activation(xn_hi[:, :, P * t:P * t + P],
                                   ln_bank(n, t)[:].rearrange("p (c q) -> p c q", c=CK), ACT.Copy)\
                       .then_inc(ln_hi, 1)

            def gu_hi(n, i, par):
                loads = i // 2 + 1 if isinstance(i, int) else None
                for j in range(2):
                    count = 16 * loads if loads is not None else (i - par) * 8 + 16
                    split_hi(F_PER * par + j, ld_f[n][F_PER * par + j], count, gu_part(wgu_hi, par, j))

            def a_projected(b):
                for j in range(2):
                    act.wait_ge(a_proj, 3 * b + j + 1)
                    act.activation(aqk_hi[:, b, j, :], bank[j][:], ACT.Identity,
                                   bias=a_bias[:, j:j + 1]).then_inc(a_qk, 1)
                    if b == 0:
                        norm(0, [TB + j])
                act.wait_ge(a_proj, 3 * b + 3)
                act.activation(a_vT[:, b, :], bank[2][:], ACT.Identity, bias=a_bias[:, 2:3])\
                   .then_inc(a_vt, 1)
                if b == 0:
                    norm(0, range(TB + 2, NT))
                act.wait_ge(a_vtr, b + 1)
                act.activation(av_hi[:, b].rearrange("p c d -> p (c d)"), bank[3][:], ACT.Copy)\
                   .then_inc(a_vh, 1)

            def a_softmax(b):
                for t in range(TB * b, TB * b + TB + 1):
                    if t < TB * b + TB:
                        act.wait_ge(a_min, t + 1)
                        act.activation(a_p[:, b, t % TB, :], a_p[:, b, t % TB, :], ACT.Exp,
                                       bias=a_nmax[:, t:t + 1], scale=-1.0,
                                       accum_out=a_sum[:, t:t + 1]).then_inc(a_exp, 1)
                    if t > TB * b:
                        act.wait_ge(a_recd, t)
                        act.activation(a_p[:, b, (t - 1) % TB, :], a_p[:, b, (t - 1) % TB, :], ACT.Copy,
                                       scale=a_rec[:, t - 1:t]).then_inc(a_norm, 1)

            def a_weighted(b):
                for kt in range(TB):
                    act.wait_ge(a_pt, TB * b + kt + 1)
                    act.activation(apt_hi[:, kt % 2, :], bank[6 + kt % 2][:], ACT.Copy).then_inc(a_pth, 1)
                act.wait_ge(a_pv, b + 1)
                act.activation(ao_hi[:, b, :], bank[0][:], ACT.Copy).then_inc(a_oh, 1)

            norm(0, range(1))
            for j in range(3):
                split_hi(j, ld_a[j], 16, a_part(aw_hi, j))
                norm(0, [j + 1])
            split_hi(3, ld_a[3], 16, a_part(aw_hi, 3))
            act.wait_ge(small_in, 32)
            a_projected(0)
            a_softmax(0)
            a_projected(1)
            a_weighted(0)
            a_softmax(1)
            gu_hi(0, 0, 0)
            a_weighted(1)

            def magnitude(slot, src, scale):
                act.activation(f_abs[:, slot, :], src, ACT.Abs, scale=scale).then_inc(f_absd, 1)
                act.activation(f_sgn[:, slot, :], src, ACT.Sign).then_inc(f_sgnd, 1)

            def ffn(n):
                def chunk(i, par, last=False):
                    done = NB * NI * n + NB * i
                    for b in range(NB):
                        act.wait_ge(f_gate, done + b + 1)
                        act.activation(f_sil[:, b, :], bank[2 * b][:], ACT.Silu, scale=1.0 / 128.0)\
                           .then_inc(f_silu, 1)
                        if b == 0 and not last:
                            need(act, f_up, done)
                            gu_hi(n, i + 1, 1 - par)
                        need(act, f_sgd, f_steps * n + NB * i + b - 1)
                        act.wait_ge(f_zd, done + b + 1)
                        magnitude(b, f_z[:, b, :], 1.0)

                norm(1 + 2 * n, range(NT - 1 if n else TB, NT))
                chunk(0, 0)
                chunk(1, 1)
                with act.Fori(1, NI // 2) as p:
                    for par in range(2):
                        chunk(2 * p + par, par)
                chunk(NI - 1, 0, last=True)
                if n == 0:
                    act.wait_ge(f_up, NB * NI)
                    for j in range(6):
                        run("w", 0, 0, j, None)
                for t in range(NT):
                    act.wait_ge(f_sgd, f_steps * n + NB * NI + t - 1)
                    act.wait_ge(f_y, NT * n + t + 1)
                    magnitude(t % 2, bank[4 + t % 2][:], 128.0)
                    if n == 0 and t >= 3:
                        norm(2, [t - 3])

            def normalize(c, k, h):
                w = P * (k + 1)
                act.wait_ge(rec_done, c + 1)
                act.activation(prob[k % 2][:, h, 0:w], prob[k % 2][:, h, 0:w], ACT.Copy,
                               scale=rec[:, k, h:h + 1]).then_inc(norm_done, 1)

            def run(what, g, b, arg, flags):
                u = NB * g + b
                if what == "ln" and arg[0] in ("c", "tail"):
                    norm(arg[1], [arg[2]])
                elif what == "gu":
                    act.wait_ge(q_done, HEADS * NB)
                    gu_hi(1, 0, 0)
                elif what == "w":
                    if arg < 6:
                        if arg < 2:
                            need(act, kv_done, 2 * u)
                        else:
                            need(act, q_done, GH * (u - 1) + arg - 1)
                    else:
                        need(act, y_done, TB * u)
                    split_hi(arg % B_RAW, ld_b[arg % B_RAW], 32 * g + 16 * (arg // B_RAW + 1),
                             w_parts(arg)[0])
                elif what == "kv_out":
                    half = arg
                    act.wait_ge(kv_done, 2 * u + half + 1)
                    if not (isinstance(u, int) and u < 2):
                        act.wait_ge(pv_done, PAIRS * (u - 2) + TRI[3] + 2 * half + 2)
                    act.activation(v_hi[:, b, 2 * half:2 * half + 2, :],
                                   bank[half][:].rearrange("p (t n) -> p t n", t=2)[:, :, P:2 * P],
                                   ACT.Copy).then_inc(vh_done, 1)
                elif what == "kt":
                    act.wait_ge(kt_done, u + 1)
                    act.activation(k1_hi[:, b, 0:P], bank[2][:, 0:P], ACT.Copy)
                    act.activation(k2_hi[:, b, P:SEQ], bank[2][:, P:SEQ], ACT.Copy).then_inc(kh_done, 1)
                elif what == "q_out":
                    h = arg
                    act.wait_ge(q_sum, GH * u + h + 1)
                    act.activation(qT_hi[:, b, h, :], rq_cos[:, h % 2, :], ACT.Copy).then_inc(q_hi, 1)
                elif what == "s":
                    k, h = arg
                    c = 16 * u + GH * k + h
                    if not (flags[0] and k == 0 and h == 0):
                        normalize(c - 1, k if h else (k - 1) % TB, (h - 1) % GH)
                    w = P * (k + 1)
                    act.wait_ge(min_done, c + 1)
                    act.activation(prob[k % 2][:, h, 0:w], prob[k % 2][:, h, 0:w], ACT.Exp,
                                   bias=nmax[:, k, h:h + 1], scale=-1.0, accum_out=esum[:, k, h:h + 1])\
                       .then_inc(exp_done, 1)
                elif what == "s_end":
                    normalize(16 * u + 15, TB - 1, GH - 1)
                elif what == "t":
                    j = PAIRS * u + TRI[arg[0]] + arg[1]
                    par = (TRI[arg[0]] + arg[1]) % 2
                    act.wait_ge(pt_done, j + 1)
                    act.activation(pt_hi[:, par, :], bank[5 + par][:], ACT.Copy).then_inc(pth_done, 1)
                elif what == "pv" and arg[0] == arg[1]:
                    act.wait_ge(pv_done, PAIRS * u + TRI[arg[0]] + arg[0] + 1)
                    act.activation(o_hi[:, arg[0] % 2].rearrange("p h q -> p (h q)"), bank[7][:], ACT.Copy)\
                       .then_inc(oh_done, 1)

            norm(1, range(TB))
            ffn(0)
            act.wait_ge(f_y, NT)
            for j in range(6, B_PER):
                run("w", 0, 0, j, None)
            walk(act, run, early=((2, 2), (3, 2)))
            ffn(1)

        @block.vector
        def _(dve):
            def x_done(n, t):
                if n == 0:
                    dve.wait_ge(x_in_sem[t], 16)
                elif n == 1:
                    dve.wait_ge(a_res, t + 1)
                elif n == 2:
                    dve.wait_ge(f_res, t + 1)
                else:
                    dve.wait_ge(y_res, TB * (NB * (KVH - 1) + t // TB) + t % TB + 1)

            def ln_stats(n, t):
                x_done(n, t)
                dve.bn_stats(stats[:, t, :], x[:, t, :]).then_inc(ln_stat, 1)
                dve.wait_ge(ln_stat, NT * n + t + 1)
                dve.bn_aggr(mv[:, t, :], stats[:, t, :]).then_inc(ln_aggr, 1)
                dve.wait_ge(ln_aggr, NT * n + t + 1)
                dve.tensor_scalar(vare[:, t, :], mv[:, t, 1:2], EPS, None, ALU.add).then_inc(ln_eps, 1)

            def ln_bn(n, t):
                x_done(n, t)
                dve.bn_stats(stats[:, t, :], x[:, t, :]).then_inc(ln_stat, 1)

            def ln_aggregate(n, t0):
                dve.wait_ge(ln_stat, NT * n + t0 + TB)
                for t in range(t0, t0 + TB):
                    dve.bn_aggr(mv[:, t, :], stats[:, t, :]).then_inc(ln_aggr, 1)
                dve.wait_ge(ln_aggr, NT * n + t0 + TB)
                dve.tensor_scalar(vare[:, t0:t0 + TB, :], mv[:, t0:t0 + TB, 1:2], EPS, None, ALU.add)\
                   .then_inc(ln_eps, TB)

            def ln_center(n, t):
                dve.wait_ge(ln_rstd, NT * n + t + 1)
                need(dve, ln_tr, NT * n + t - 1)
                dve.tensor_scalar(xn_tmp[:, t % 2, :], x[:, t, :], mv[:, t, 0:1], rstd[:, t, 0:1],
                                  ALU.subtract, ALU.mult).then_inc(ln_xn, 1)

            def ln_rest(n, t):
                dve.wait_ge(ln_hi, NT * n + t + 1)
                dve.tensor_tensor(xn_lo[:, :, P * t:P * t + P],
                                  ln_bank(n, t)[:].rearrange("p (c q) -> p c q", c=CK),
                                  xn_hi[:, :, P * t:P * t + P].bitcast(F32), ALU.subtract)\
                   .then_inc(ln_lo, 1)

            def a_projected(b):
                for j in range(2):
                    dve.wait_ge(a_qk, 2 * b + j + 1)
                    dve.scalar_tensor_tensor(out=aqk_lo[:, b, j, :], in0=bank[j][:],
                                             scalar=a_bias[:, j:j + 1],
                                             in1=aqk_hi[:, b, j, :].bitcast(F32),
                                             op0=ALU.add, op1=ALU.subtract).then_inc(a_lo, 1)
                    if b == 0:
                        ln_rest(0, TB + j)
                        ln_center(0, TB + 2 + j)
                if b == 0:
                    for t in range(TB + 2, NT):
                        ln_rest(0, t)
                dve.wait_ge(a_vh, b + 1)
                dve.tensor_tensor(av_lo[:, b].rearrange("p c d -> p (c d)"), bank[3][:],
                                  av_hi[:, b].rearrange("p c d -> p (c d)").bitcast(F32),
                                  ALU.subtract).then_inc(a_v, 1)

            def a_softmax(b):
                for t in range(TB * b, TB * b + TB + 1):
                    if t < TB * b + TB:
                        dve.wait_ge(a_s, t + 1)
                        dve.tensor_scalar(a_p[:, b, t % TB, :], bank[4 + t % 2][:], -SCALE, None,
                                          ALU.mult, ALU.min, accum_out=a_nmax[:, t:t + 1])\
                           .then_inc(a_min, 1)
                    if t > TB * b:
                        dve.wait_ge(a_exp, t)
                        dve.reciprocal(a_rec[:, t - 1:t], a_sum[:, t - 1:t]).then_inc(a_recd, 1)

            def a_weighted(b):
                for kt in range(TB):
                    if b and kt:
                        ln_bn(1, kt - 1)
                    dve.wait_ge(a_pth, TB * b + kt + 1)
                    dve.tensor_tensor(apt_lo[:, kt % 2, :], bank[6 + kt % 2][:],
                                      apt_hi[:, kt % 2, :].bitcast(F32), ALU.subtract).then_inc(a_ptl, 1)
                dve.wait_ge(a_oh, b + 1)
                dve.tensor_tensor(ao_lo[:, b, :], bank[0][:], ao_hi[:, b, :].bitcast(F32),
                                  ALU.subtract).then_inc(a_ol, 1)

            def a_residual(*tiles):
                for t in tiles:
                    dve.wait_ge(a_bod, t + 1)
                    dve.wait_ge(a_y, t + 1)
                    dve.tensor_tensor(x[:, t, :], a_y_bank(t)[:], x[:, t, :], ALU.add)\
                       .then_inc(a_res, 1)

            for t in range(TB + 4):
                if t < TB:
                    ln_stats(0, t)
                if 0 < t <= TB:
                    ln_center(0, t - 1)
                if t >= 4:
                    ln_rest(0, t - 4)
            for t in range(TB, NT):
                ln_bn(0, t)
            ln_aggregate(0, TB)
            ln_center(0, TB)
            ln_center(0, TB + 1)
            dve.wait_ge(small_in, 32)
            a_projected(0)
            a_softmax(0)
            a_projected(1)
            a_weighted(0)
            a_softmax(1)
            a_residual(0, 1, 2, 3)
            a_weighted(1)
            ln_bn(1, 3)
            ln_aggregate(1, 0)
            a_residual(4, 5)
            ln_center(1, 0)
            ln_center(1, 1)
            a_residual(6)
            for t in range(TB):
                ln_rest(1, t)
                if t < 2:
                    ln_center(1, t + 2)
                if t == 1:
                    a_residual(7)
            for t in range(TB, NT):
                ln_bn(1, t)
            ln_aggregate(1, TB)
            for t in range(TB, NT + 1):
                if t < NT:
                    ln_center(1, t)
                if t > TB:
                    ln_rest(1, t - 1)

            def truncate(count, slot):
                dve.wait_ge(f_absd, count)
                dve.tensor_scalar(f_rnd[:, slot, :], f_abs[:, slot, :], 128.0, ROUND, ALU.min, ALU.add)\
                   .then_inc(f_rndd, 1)
                dve.wait_ge(f_rndd, count)
                dve.scalar_tensor_tensor(out=f_off[:, slot, :], in0=f_rnd[:, slot, :], scalar=ROUND,
                                         in1=f_abs[:, slot, :], op0=ALU.subtract, op1=ALU.is_gt)\
                   .then_inc(f_offd, 1)
                dve.wait_ge(f_offd, count)
                dve.wait_ge(f_sgnd, count)
                dve.scalar_tensor_tensor(out=f_val[:, slot, :], in0=f_rnd[:, slot, :], scalar=ROUND,
                                         in1=f_off[:, slot, :], op0=ALU.subtract, op1=ALU.subtract)\
                   .then_inc(f_vald, 1)

            def ffn(n):
                def down_split(i, par):
                    count = 16 * (i // 2 + 1) if isinstance(i, int) else (i - par) * 8 + 16
                    dve.wait_ge(ld_f[n][F_PER * par + 2], count)
                    dve.tensor_scalar(wd_hi[:, i, :], raw[:, F_PER * par + 2, :], 1.0, None, ALU.mult)\
                       .then_inc(wd_h, 1)
                    dve.wait_ge(wd_h, NI * n + i + 1)
                    dve.tensor_tensor(wd_lo[:, i, :], raw[:, F_PER * par + 2, :],
                                      wd_hi[:, i, :].bitcast(F32), ALU.subtract).then_inc(wd_done, 1)

                def quantized(i, b):
                    dve.wait_ge(f_sgd, f_steps * n + NB * i + b + 1)
                    dve.tensor_scalar(inner[:, i, b, :], f_val[:, b, :], 127.0, None, ALU.min)\
                       .then_inc(f_qd, 1)

                def chunk(i, par):
                    for b in range(NB):
                        done = NB * NI * n + NB * i + b
                        dve.wait_ge(f_silu, done + 1)
                        dve.wait_ge(f_up, done + 1)
                        dve.tensor_tensor(f_z[:, b, :], bank[2 * b + 1][:], f_sil[:, b, :], ALU.mult)\
                           .then_inc(f_zd, 1)
                        if b == 0:
                            if not (isinstance(i, int) and i == 0):
                                quantized(i - 1, 1)
                            down_split(i, par)
                        else:
                            quantized(i, 0)
                        truncate(f_steps * n + NB * i + b + 1, b)

                chunk(0, 0)
                chunk(1, 1)
                with dve.Fori(1, NI // 2) as p:
                    for par in range(2):
                        chunk(2 * p + par, par)
                chunk(NI - 1, 0)
                quantized(NI - 1, 1)

                def add(t):
                    dve.wait_ge(f_sgd, f_steps * n + NB * NI + t + 1)
                    dve.scalar_tensor_tensor(out=x[:, t, :], in0=f_val[:, t % 2, :], scalar=127.0,
                                             in1=x[:, t, :], op0=ALU.min, op1=ALU.add).then_inc(f_res, 1)

                for t in range(NT + 1):
                    if n == 0 and 2 <= t:
                        ln_center(2, t - 2)
                    if n == 0 and 4 <= t:
                        ln_rest(2, t - 4)
                    if t < NT:
                        truncate(f_steps * n + NB * NI + t + 1, t % 2)
                    if t:
                        add(t - 1)
                        if n == 0:
                            ln_stats(2, t - 1)

            def run(what, g, b, arg, flags):
                u = NB * g + b
                if what == "ln":
                    stage, n, t = arg
                    if stage == "a":
                        ln_stats(n, t)
                    elif stage == "b":
                        ln_center(n, t)
                    elif stage == "c":
                        ln_rest(n, t)
                    elif stage == "tail":
                        if t == 5:
                            ln_center(n, 7)
                        ln_rest(n, t)
                elif what == "kv_out":
                    half = arg
                    ps = bank[half][:].rearrange("p (t n) -> p t n", t=2)
                    ts = slice(2 * half, 2 * half + 2)
                    dve.wait_ge(vh_done, 2 * u + half + 1)
                    if half == 0:
                        need(dve, kt_done, u)
                        if isinstance(u, int) and u == 0:
                            dve.wait_ge(ln_tr, 3 * NT)
                    dve.tensor_tensor(rk_cos[:, ts, :], ps[:, :, 0:P], tab_k[:, 0, ts, :], ALU.mult)
                    dve.tensor_tensor(rk_sin[:, ts, 0:P // 2], ps[:, :, P // 2:P],
                                      tab_k[:, 1, ts, 0:P // 2], ALU.mult)
                    dve.tensor_tensor(rk_sin[:, ts, P // 2:P], ps[:, :, 0:P // 2],
                                      tab_k[:, 1, ts, P // 2:P], ALU.mult).then_inc(kv_rot, 1)
                    dve.tensor_tensor(v_lo[:, b, ts, :], ps[:, :, P:2 * P],
                                      v_hi[:, b, ts, :].bitcast(F32), ALU.subtract).then_inc(v_done, 1)
                elif what == "kt":
                    dve.wait_ge(kh_done, u + 1)
                    dve.tensor_tensor(k2_tmp[:], bank[2][:, 0:P], colscale, ALU.mult).then_inc(k2_scaled, 1)
                    dve.tensor_tensor(k1_lo[:, b, 0:P], bank[2][:, 0:P], k1_hi[:, b, 0:P].bitcast(F32),
                                      ALU.subtract)
                    dve.wait_ge(k2_scaled, u + 1)
                    dve.tensor_copy(k2_hi[:, b, 0:P], k2_tmp[:]).then_inc(k2_round, 1)
                    dve.tensor_tensor(k2_lo[:, b, P:SEQ], bank[2][:, P:SEQ],
                                      k2_hi[:, b, P:SEQ].bitcast(F32), ALU.subtract)
                    dve.wait_ge(k2_round, u + 1)
                    dve.tensor_tensor(k2_lo[:, b, 0:P], k2_tmp[:], k2_hi[:, b, 0:P].bitcast(F32),
                                      ALU.subtract).then_inc(k_done, 1)
                elif what == "q" and arg[1] == 1:
                    h = arg[0]
                    ps = bank[q_bank(u, h)]
                    half = P // 2
                    dve.wait_ge(q_done, GH * u + h + 1)
                    need(dve, q_lo, GH * u + h - 1)
                    dve.tensor_tensor(rq_cos[:, h % 2, :], ps[:], tab_q[:, 0, :], ALU.mult)
                    dve.tensor_tensor(rq_sin[0:half, h % 2, :], ps[half:P, :], tab_q[half:P, 1, :], ALU.mult)
                    dve.tensor_tensor(rq_sin[half:P, h % 2, :], ps[0:half, :], tab_q[0:half, 1, :],
                                      ALU.mult).then_inc(q_read, 1)
                elif what == "q_out" and isinstance(u, int) and u == 0:
                    dve.wait_ge(q_hi, arg + 1)
                    dve.tensor_tensor(qT_lo[:, b, arg, :], rq_cos[:, arg % 2, :],
                                      qT_hi[:, b, arg, :].bitcast(F32), ALU.subtract).then_inc(q_lo, 1)
                elif what == "s":
                    k, h = arg
                    c = 16 * u + GH * k + h
                    w = P * (k + 1)
                    p_out = prob[k % 2][:, h, 0:w]
                    dve.wait_ge(s_done, c + 1)
                    src = bank[3 + h % 2][:, 0:w]
                    if k == 0:
                        dve.tensor_tensor(p_out, src, rowscale, ALU.mult).then_inc(s_scaled, 1)
                        dve.wait_ge(s_scaled, GH * u + h + 1)
                        src = p_out
                    if not (flags[0] and k == 0 and h == 0):
                        sums(c - 1, k if h else (k - 1) % TB, (h - 1) % GH)
                    dve.tensor_tensor_reduce(p_out, src, causal[:, 512 - w:512], -SCALE, -LOWEST,
                                             ALU.add, ALU.min, nmax[:, k, h:h + 1]).then_inc(min_done, 1)
                elif what == "s_end":
                    sums(16 * u + 15, TB - 1, GH - 1)
                elif what == "t":
                    j = PAIRS * u + TRI[arg[0]] + arg[1]
                    par = (TRI[arg[0]] + arg[1]) % 2
                    dve.wait_ge(pth_done, j + 1)
                    dve.tensor_tensor(pt_lo[:, par, :], bank[5 + par][:], pt_hi[:, par, :].bitcast(F32),
                                      ALU.subtract).then_inc(ptl_done, 1)
                elif what == "pv" and arg[0] == arg[1]:
                    dve.wait_ge(oh_done, TB * u + arg[0] + 1)
                    dve.tensor_tensor(o_lo[:, arg[0] % 2].rearrange("p h q -> p (h q)"), bank[7][:],
                                      o_hi[:, arg[0] % 2].rearrange("p h q -> p (h q)").bitcast(F32),
                                      ALU.subtract).then_inc(ol_done, 1)
                elif what == "y":
                    dve.wait_ge(y_done, TB * u + arg + 1)
                    t = TB * b + arg
                    dve.tensor_tensor(x[:, t, :], bank[Y_BANK[arg]][:], x[:, t, :], ALU.add)\
                       .then_inc(y_res, 1)

            def sums(c, k, h):
                dve.wait_ge(exp_done, c + 1)
                dve.reciprocal(rec[:, k, h:h + 1], esum[:, k, h:h + 1]).then_inc(rec_done, 1)

            ffn(0)
            dve.wait_ge(table_in, 48)
            dve.wait_ge(f_y, NT)
            for w in (k1_hi, k1_lo):
                for b in range(NB):
                    dve.memset(w[:, b, P:2 * P].bitcast(F32), 0.0).then_inc(k1_zero, 1)
            walk(dve, run)
            ln_stats(3, NT - 1)
            ln_center(3, NT - 1)
            ln_rest(3, NT - 1)
            ffn(1)

        @block.tensor
        def _(pe):
            def product(out_ap, terms, start=True, stop=True):
                n = len(terms)
                for i, (s_hi, s_lo, m_hi, m_lo) in enumerate(terms):
                    pe.matmul(out_ap, s_lo, m_hi, start=start and i == 0, stop=False)
                    pe.matmul(out_ap, s_hi, m_lo, start=False, stop=False)
                    r = pe.matmul(out_ap, s_hi, m_hi, start=False, stop=stop and i == n - 1)
                return r

            def staged(out_ap, hi_terms, lo_terms, lo_ready, start=True, stop=True):
                for i, (a, b) in enumerate(hi_terms):
                    pe.matmul(out_ap, a, b, start=start and i == 0, stop=False)
                pe.wait_ge(*lo_ready)
                for i, (a, b) in enumerate(lo_terms):
                    r = pe.matmul(out_ap, a, b, start=False, stop=stop and i == len(lo_terms) - 1)
                return r

            def norm(n, tiles):
                for t in tiles:
                    pe.wait_ge(ln_xn, NT * n + t + 1)
                    need(pe, ln_lo, NT * n + t - (0 if n == 3 and t < TB else 1))
                    for c in range(CK):
                        r = pe.transpose(ln_bank(n, t)[:, P * c:P * c + P],
                                         xn_tmp[:, t % 2, P * c:P * c + P], ident[:])
                    r.then_inc(ln_tr, 1)

            def a_projected(b):
                cols = slice(SEQ * b, SEQ * b + SEQ)
                pe.wait_ge(ln_lo, TB * (b + 1))
                for j in range(3):
                    pe.wait_ge(lo_done, j + 1)
                    if b:
                        pe.wait_ge(*((a_lo, j + 1) if j < 2 else (a_vt, 1)))
                    product(bank[j][:], [(aw_hi[:, j, c, :], aw_lo[:, j, c, :], xn_hi[:, c, cols],
                                          xn_lo[:, c, cols]) for c in range(CK)]).then_inc(a_proj, 1)
                    if b == 0:
                        norm(0, range(TB + j, TB + j + (2 if j == 2 else 1)))

            def a_values(b):
                pe.wait_ge(a_vt, b + 1)
                need(pe, a_v, b)
                for kt in range(TB):
                    r = pe.transpose(bank[3][:, P * kt:P * kt + P], a_vT[:, b, P * kt:P * kt + P], ident[:])
                r.then_inc(a_vtr, 1)

            def a_scores(b):
                pe.wait_ge(a_lo, 2 * b + 2)
                for t in range(TB * b, TB * b + TB):
                    need(pe, a_min, t - 1)
                    q = slice(P * (t % TB), P * (t % TB) + P)
                    product(bank[4 + t % 2][:], [(aqk_hi[:, b, 0, q], aqk_lo[:, b, 0, q],
                                                  aqk_hi[:, b, 1, :], aqk_lo[:, b, 1, :])])\
                        .then_inc(a_s, 1)

            def a_weighted(b):
                pe.wait_ge(a_norm, TB * b + TB)
                pe.wait_ge(a_v, b + 1)

                def turn(kt):
                    need(pe, a_ptl, TB * b + kt - 1)
                    for qb in range(TB):
                        r = pe.transpose(bank[6 + kt % 2][:, P * qb:P * qb + P],
                                         a_p[:, b, qb, P * kt:P * kt + P], ident[:])
                    r.then_inc(a_pt, 1)

                turn(0)
                for kt in range(TB):
                    if kt + 1 < TB:
                        turn(kt + 1)
                    pe.wait_ge(a_pth, TB * b + kt + 1)
                    if kt == 0:
                        pe.wait_ge(a_lo, 4)
                        need(pe, a_res, TB * b)
                    p_hi, p_lo = apt_hi[:, kt % 2, :], apt_lo[:, kt % 2, :]
                    r = staged(bank[0][:], [(av_lo[:, b, kt, :], p_hi), (av_hi[:, b, kt, :], p_hi)],
                               [(av_hi[:, b, kt, :], p_lo)], (a_ptl, TB * b + kt + 1),
                               start=kt == 0, stop=kt == TB - 1)
                r.then_inc(a_pv, 1)

            def a_output(b):
                pe.wait_ge(a_oh, b + 1)
                pe.wait_ge(lo_done, A_PIECES)
                pe.wait_ge(a_v, NB)
                need(pe, a_res, TB * b)
                for t in range(TB * b, TB * b + TB):
                    q = slice(P * (t % TB), P * (t % TB) + P)
                    staged(a_y_bank(t)[:], [(ao_hi[:, b, q], a_part(w, 3)) for w in (aw_lo, aw_hi)],
                           [(ao_lo[:, b, q], a_part(aw_hi, 3))], (a_ol, b + 1)).then_inc(a_y, 1)

            pe.wait_ge(ident_ready, 1)
            norm(0, range(TB))
            a_projected(0)
            a_values(0)
            a_scores(0)
            a_projected(1)
            a_values(1)
            a_weighted(0)
            a_scores(1)
            a_output(0)
            a_weighted(1)
            a_output(1)
            norm(1, range(TB))

            def ffn(n):
                def chunk(i, par):
                    for b in range(NB):
                        cols = slice(SEQ * b, SEQ * b + SEQ)
                        done = NB * NI * n + NB * i + b
                        if b == 0:
                            pe.wait_ge(lo_done, lo_f[n] + 2 * i + 2)
                        need(pe, f_zd, done - 1)
                        if isinstance(i, int) and i == 0:
                            pe.wait_ge(ln_lo, NT * (1 + 2 * n) + TB * (b + 1))
                        for j in range(2):
                            terms = [(wgu_hi[:, par, j, c, :], wgu_lo[:, par, j, c, :], xn_hi[:, c, cols],
                                      xn_lo[:, c, cols]) for c in range(CK)]
                            if isinstance(i, int) and i == 0 and b == 0 and j == 1:
                                product(bank[1][:], terms[:2], stop=False)
                                norm(1 + 2 * n, [NT - 1 if n else TB])
                                product(bank[1][:], terms[2:], start=False).then_inc(f_up, 1)
                                norm(1 + 2 * n, range(NT if n else TB + 1, NT))
                            else:
                                product(bank[2 * b + j][:], terms).then_inc((f_gate, f_up)[j], 1)

                chunk(0, 0)
                chunk(1, 1)
                with pe.Fori(1, NI // 2) as p:
                    for par in range(2):
                        chunk(2 * p + par, par)
                chunk(NI - 1, 0)
                pe.wait_ge(wd_done, NI * (n + 1) - 1)
                pe.wait_ge(f_qd, NB * NI * (n + 1) - 3)
                for t in range(NT):
                    b, q = t // TB, slice(P * (t % TB), P * (t % TB) + P)
                    if t:
                        pe.wait_ge(f_qd, NB * NI * (n + 1) - 1 + b)
                    if t > 1:
                        pe.wait_ge(f_sgnd, f_steps * n + NB * NI + t - 1)
                    for i in range(NI):
                        if t == 0 and i == NI - 1:
                            pe.wait_ge(wd_done, NI * (n + 1))
                            pe.wait_ge(f_qd, NB * NI * (n + 1) - 1)
                        pe.matmul(bank[4 + t % 2][:], inner[:, i, b, q], wd_lo[:, i, :], start=i == 0,
                                  stop=False)
                        r = pe.matmul(bank[4 + t % 2][:], inner[:, i, b, q], wd_hi[:, i, :], start=False,
                                      stop=i == NI - 1)
                    r.then_inc(f_y, 1)
                    if n == 0 and t >= 3:
                        norm(2, [t - 3])

            def run(what, g, b, arg, flags):
                u = NB * g + b
                first, last = flags
                start_up = isinstance(u, int) and u == 0
                if what == "ln":
                    if arg[0] in ("t", "tail"):
                        if arg[1] == 3 and arg[2] >= TB:
                            pe.wait_ge(min_done, 16 * NB * KVH)
                        norm(arg[1], [arg[2]])
                elif what == "kv":
                    t = arg
                    if t == 0 and isinstance(u, int) and u < 2:
                        pe.wait_ge(ln_lo, 2 * NT + TB * (u + 1))
                    if t == 0:
                        pe.wait_ge(lo_done, lo_b + B_PER * g + 2)
                    if t == 0 and not (isinstance(u, int) and u < 2):
                        pe.wait_ge(y_res, TB * (u - 2) + 1)
                    if t == 2:
                        need(pe, q_read, GH * u)
                    tok = slice(SEQ * b + P * t, SEQ * b + P * t + P)
                    r = product(bank[t // 2][:, 2 * P * (t % 2):2 * P * (t % 2) + 2 * P],
                                [(xn_hi[:, c, tok], xn_lo[:, c, tok], wkv_hi[:, c, :], wkv_lo[:, c, :])
                                 for c in range(CK)])
                    if t % 2:
                        r.then_inc(kv_done, 1)
                elif what == "q":
                    h, half = arg
                    if half == 0:
                        pe.wait_ge(lo_done, lo_b + B_PER * g + 3 + h)
                        if start_up:
                            if h == 3:
                                pe.wait_ge(ln_lo, 3 * NT)
                        elif h < 2:
                            pe.wait_ge(v_done, 2 * u + h + 1)
                        elif h == 2:
                            pe.wait_ge(k_done, u + 1)
                        else:
                            pe.wait_ge(y_res, TB * (u - 1) + 2)
                    cols = slice(SEQ * b, SEQ * b + SEQ)
                    r = product(bank[q_bank(u, h)][:],
                                [(wq_hi[:, h, c, :], wq_lo[:, h, c, :], xn_hi[:, c, cols], xn_lo[:, c, cols])
                                 for c in (2 * half, 2 * half + 1)], start=half == 0, stop=half == 1)
                    if half:
                        r.then_inc(q_done, 1)
                elif what == "kt":
                    pe.wait_ge(kv_rope, u + 1)
                    if not (isinstance(u, int) and u < 2):
                        pe.wait_ge(y_res, TB * (u - 1))
                    for t in range(TB):
                        r = pe.transpose(bank[2][:, P * t:P * t + P], rk_cos[:, t, :], ident[:])
                    r.then_inc(kt_done, 1)
                elif what == "s":
                    k, h = arg
                    c = 16 * u + GH * k + h
                    if k == 0 and h == 0:
                        pe.wait_ge(k_done, u + 1)
                        if start_up:
                            pe.wait_ge(k1_zero, 2 * NB)
                    if k == 0:
                        pe.wait_ge(q_lo, GH * u + h + 1)
                    need(pe, min_done, c - 1)
                    q = slice(P * k, P * k + P)
                    w = max(2, k + 1) * P
                    keys = (k1_hi[:, b, :], k1_lo[:, b, :]) if k == 0 else (k2_hi[:, b, 0:w], k2_lo[:, b, 0:w])
                    product(bank[3 + h % 2][:, 0:w], [(qT_hi[:, b, h, q], qT_lo[:, b, h, q], *keys)])\
                        .then_inc(s_done, 1)
                elif what == "t":
                    k, kt = arg
                    if kt == 0:
                        pe.wait_ge(norm_done, 16 * u + GH * k + GH)
                    par = (TRI[k] + kt) % 2
                    need(pe, ptl_done, PAIRS * u + TRI[k] + kt - 1)
                    for h in range(GH):
                        r = pe.transpose(bank[5 + par][:, P * h:P * h + P],
                                         prob[k % 2][:, h, P * kt:P * kt + P], ident[:])
                    r.then_inc(pt_done, 1)
                elif what == "pv":
                    k, kt = arg
                    par = (TRI[k] + kt) % 2
                    pe.wait_ge(pth_done, PAIRS * u + TRI[k] + kt + 1)
                    if kt == 0:
                        need(pe, ol_done, TB * u + k)
                    staged(bank[7][:], [(v_lo[:, b, kt, :], pt_hi[:, par, :]),
                                        (v_hi[:, b, kt, :], pt_hi[:, par, :])],
                           [(v_hi[:, b, kt, :], pt_lo[:, par, :])],
                           (ptl_done, PAIRS * u + TRI[k] + kt + 1), start=kt == 0, stop=kt == k)\
                        .then_inc(pv_done, 1)
                elif what == "y":
                    k = arg
                    pe.wait_ge(oh_done, TB * u + k + 1)
                    if k == 0 and b == 0:
                        pe.wait_ge(lo_done, lo_b + B_PER * g + B_PER)
                    if last and k < 2:
                        pe.wait_ge(y_res, TB * u)
                        if k == 1:
                            pe.wait_ge(ln_lo, 3 * NT + TB)
                    elif k == 0:
                        pe.wait_ge(q_read, GH * (u + 1) + 1)
                    elif k == 1:
                        pe.wait_ge(q_read, GH * (u + 1) + 2)
                    elif k == 2:
                        if not last:
                            pe.wait_ge(q_read, GH * (u + 1) + 3)
                    else:
                        pe.wait_ge(y_res, TB * u + 3)
                    staged(bank[Y_BANK[k]][:],
                           [(o_hi[:, k % 2, h, :], w[:, h, :]) for h in range(GH) for w in (wo_lo, wo_hi)],
                           [(o_lo[:, k % 2, h, :], wo_hi[:, h, :]) for h in range(GH)],
                           (ol_done, TB * u + k + 1)).then_inc(y_done, 1)

            ffn(0)
            walk(pe, run)
            ffn(1)


Q_BANK = [0, 1, 2, 1]
Y_BANK = [0, 1, 2, 2]


def tables():
    inv = (np.float32(1.0) / np.float32(10000.0) ** (np.arange(0, P, 2, dtype=np.float32) / np.float32(P)))
    ang = np.arange(SEQ, dtype=np.float32)[:, None] * inv[None, :].astype(np.float32)
    emb = np.concatenate([ang, ang], axis=1)
    cos, sin = np.cos(emb).astype(np.float32), np.sin(emb).astype(np.float32)
    signed = np.concatenate([-sin[:, :P // 2], sin[:, P // 2:]], axis=1)
    swapped = np.concatenate([signed[:, P // 2:], signed[:, :P // 2]], axis=1)
    rope_q = np.ascontiguousarray(np.stack([cos.T, swapped.T], axis=1))
    rope_k = np.stack([cos, signed]).reshape(2, TB, P, P).transpose(2, 0, 1, 3)
    q, k = np.arange(P)[:, None], np.arange(P)[None, :]
    causal = np.zeros((P, 4 * P), np.float32)
    causal[:, 3 * P:] = np.where(q >= k, 0.0, LOWEST)
    keys = np.where(k < SYS, 0.5, np.where(k < BOOST, 1.5, 1.0))
    rows = np.where(q >= BOOST, keys, 1.0)
    masks = np.concatenate([causal, rows, np.broadcast_to(keys, (P, P))], axis=1)
    return rope_q, np.ascontiguousarray(rope_k), np.ascontiguousarray(masks.astype(np.float32))


def kernel(**inputs):
    import concourse.bacc as bacc
    from concourse.bass_utils import run_bass_kernel_spmd

    a = {k.removeprefix("L0_"): np.asarray(v) for k, v in inputs.items()}
    pad = NI * P - INTER

    def columns(w, n):
        return w.reshape(CK, P, n, P).transpose(2, 1, 0, 3).reshape(n, P, CK * P)

    gate = columns(np.pad(a["ffn_w_gate"], ((0, pad), (0, 0))).T, NI)
    up = columns(np.pad(a["ffn_w_up"], ((0, pad), (0, 0))).T, NI)
    down = np.pad(a["ffn_w_down"], ((0, 0), (0, pad))).T.reshape(NI, P, C)
    ffn = np.stack([gate, up, down], axis=1).reshape(NI * F_PER, P, C)
    kv = np.stack([a["attn_b_wk"].reshape(KVH, P, C), a["attn_b_wv"].reshape(KVH, P, C)], axis=1)
    kv = kv.reshape(KVH, 2, P, 2, 2, P).transpose(0, 3, 5, 4, 1, 2).reshape(KVH, 2, P, C)
    wq = columns(a["attn_b_wq"].T, HEADS).reshape(KVH, GH, P, C)
    wo = a["attn_b_wo"].T.reshape(KVH, GH, P, C)
    att = np.concatenate([kv, wq, wo], axis=1).reshape(KVH * B_PER, P, C)
    weights = np.concatenate([columns(a["attn_a_Wqkv"], 3), a["attn_a_Wo"][None], ffn, att])
    rope_q, rope_k, masks = tables()
    arrays = {
        "x": np.ascontiguousarray(a["attn_a_x"]),
        "weights": np.ascontiguousarray(weights),
        "bqkv": np.ascontiguousarray(a["attn_a_bqkv"].reshape(3, P).T),
        "bo": np.ascontiguousarray(np.broadcast_to(a["attn_a_bo"], (P, C))),
        "rope_q": rope_q, "rope_k": rope_k, "masks": masks,
    }
    nc = bacc.Bacc("TRN2", target_bir_lowering=False, num_devices=1)
    args = [nc.dram_tensor(n, v.shape, mybir.dt.from_np(v.dtype), kind="ExternalInput").ap()
            for n, v in arrays.items()]
    out = nc.dram_tensor("out", a["attn_a_x"].shape, F32, kind="ExternalOutput").ap()
    build(nc, *args, out)
    return run_bass_kernel_spmd(nc, [arrays], core_ids=[0]).results[0]["out"]
```
